# Optimizing a Trainium2 kernel written in Bass

```python
import numpy as np
import jax
import jax.numpy as jnp

def _softmax(x, axis=-1):
    return jax.nn.softmax(x, axis=axis)

def _gelu(x):
    return jax.nn.gelu(x, approximate=True)

def _silu(x):
    return jax.nn.silu(x)

def _sigmoid(x):
    return jax.nn.sigmoid(x)

def _layernorm(x, axis=-1, eps=1e-05):
    m = jnp.mean(x, axis=axis, keepdims=True)
    v = jnp.var(x, axis=axis, keepdims=True)
    return (x - m) / jnp.sqrt(v + eps)

def _scatter_add(tgt, idx, src, axis=0):
    return tgt.at[idx].add(src)

def _segment_sum(src, seg, n):
    return jax.ops.segment_sum(src, seg, n)
kernel_name = 'mk_xattn_ffn_d1_seqx_r2_d0a17a'

def setup_inputs(seed: int=0):
    np.random.seed(seed)
    _w = jnp.asarray

    def _rec_inputs():
        import jax
        import jax.numpy as jnp
        _rk = jax.random.key(seed)
        x = -0.000125 + 0.9999 * jax.random.normal(jax.random.fold_in(_rk, 1), (4, 1024, 1024), jnp.float32)
        _lenS = 1024 - jax.random.randint(jax.random.fold_in(_rk, 7), (4,), 0, max(1, 1024 // 4) + 1, jnp.int32)
        _lenS2 = 1024 - jax.random.randint(jax.random.fold_in(_rk, 8), (4,), 0, max(1, 1024 // 4) + 1, jnp.int32)
        _ctx_2048P = jax.random.normal(jax.random.fold_in(_rk, 11), (4, 16, 1024), jnp.float32)
        _ctx_2048c = jax.random.dirichlet(jax.random.fold_in(_rk, 511), 0.3 * jnp.ones((16,), jnp.float32), (4, 1024))
        _ctx_2048t = jnp.einsum('bsk,bkd->bsd', _ctx_2048c, _ctx_2048P)
        _ctx_2048t = _ctx_2048t * jax.lax.rsqrt(jnp.mean(jnp.square(_ctx_2048t)) + 1e-12) * 0.953939
        ctx_2048 = -0.00010331 + 0.999899 * (_ctx_2048t + 0.3 * jax.random.normal(jax.random.fold_in(_rk, 611), (4, 1024, 1024), jnp.float32))
        _validS = jnp.arange(1024)[None, :] < _lenS[:, None]
        _validS2 = jnp.arange(1024)[None, :] < _lenS2[:, None]
        _causal = jnp.tril(jnp.ones((1024, 1024), dtype=bool))
        mask_Bx1xS2_ff0 = jnp.where(jnp.ones((4, 1, 1024), dtype=bool), 0.0, -1000000000.0).astype(jnp.float32)
        return (x, ctx_2048, mask_Bx1xS2_ff0)
    x, ctx_2048, mask_Bx1xS2_ff0 = _rec_inputs()

    def _L0_xattn_setup():
        import jax, jax.numpy as jnp
        import numpy as np
        FP8_E4M3_MAX = 448.0
        EPS = 1e-12

        def _fp8_quant_dequant(x):
            amax = jnp.max(jnp.abs(x))
            scale = FP8_E4M3_MAX / jnp.maximum(amax, EPS)
            q = jnp.clip(x * scale, -FP8_E4M3_MAX, FP8_E4M3_MAX).astype(jnp.float8_e4m3fn)
            return q.astype(jnp.float32) / scale
        key = jax.random.key(seed)
        k1, k2 = jax.random.split(key)
        B, M, K, N = (32, 256, 1024, 1024)
        inp = jax.random.normal(k1, (B, M, K), dtype=jnp.float32)
        weight = jax.random.normal(k2, (B, K, N), dtype=jnp.float32)
        bias = jnp.zeros((B, 1, N), dtype=jnp.float32)
        return {'input': inp, 'weight': weight, 'bias': bias}
    _L0_xattn_all = _L0_xattn_setup()
    _L0_xattn_in = {k: v for k, v in _L0_xattn_all.items() if k in ()}
    del _L0_xattn_all

    def _L0_ffn_setup():
        import math
        import jax, jax.numpy as jnp
        import numpy as np
        from jax import lax
        D = 1024
        I = 512
        E = 32
        K = 4
        NG = 8
        TKG = 3
        NSH = 2
        SCALE = 2.5
        CF = 1.25
        B, S = (2, 1024)

        def _router(x, router_w, e_bias):
            scores = jax.nn.sigmoid(x @ router_w.T)
            sc = scores + e_bias[None, :]
            T = x.shape[0]
            gs = sc.reshape(T, NG, E // NG)
            group_scores = lax.top_k(gs, 2)[0].sum(-1)
            _, gidx = lax.top_k(group_scores, TKG)
            gmask = jnp.zeros((T, NG), sc.dtype).at[jnp.arange(T)[:, None], gidx].set(1.0)
            smask = jnp.repeat(gmask, E // NG, axis=1)
            masked = jnp.where(smask > 0, sc, 0.0)
            _, topk_idx = lax.top_k(masked, K)
            topk_w = jnp.take_along_axis(scores, topk_idx, axis=1)
            topk_w = topk_w / (topk_w.sum(-1, keepdims=True) + 1e-20)
            topk_w = topk_w * SCALE
            return (topk_idx.astype(jnp.int32), topk_w)

        def _moe_forward(hidden_states, router_w, e_bias, W_gate, W_up, W_down, shared_gate, shared_up, shared_down):
            b, s, d = hidden_states.shape
            T = b * s
            C = int(math.ceil(CF * T / E))
            EC = E * C
            x = hidden_states.reshape(T, d)
            topk_idx, topk_w = _router(x, router_w, e_bias)
            expert_flat = topk_idx.reshape(-1)
            w_flat = topk_w.reshape(-1)
            tok_flat = jnp.repeat(jnp.arange(T, dtype=jnp.int32), K)
            sort_ix = jnp.argsort(expert_flat)
            e_sorted = expert_flat[sort_ix]
            tok_s = tok_flat[sort_ix]
            w_s = w_flat[sort_ix]
            counts = jnp.zeros(E, jnp.int32).at[e_sorted].add(1)
            group_start = jnp.concatenate([jnp.zeros(1, jnp.int32), jnp.cumsum(counts)[:-1].astype(jnp.int32)])
            pos = jnp.arange(T * K, dtype=jnp.int32) - group_start[e_sorted]
            valid = pos < C
            dest = e_sorted * C + jnp.where(valid, pos, 0)
            slots_token = jnp.zeros(EC, jnp.int32).at[dest].add(jnp.where(valid, tok_s, 0))
            slots_w = jnp.zeros(EC, w_s.dtype).at[dest].add(jnp.where(valid, w_s, 0.0))
            Xp = x[slots_token].reshape(E, C, d)
            G = jnp.einsum('ecd,edi->eci', Xp, W_gate)
            U = jnp.einsum('ecd,edi->eci', Xp, W_up)
            Y = jnp.einsum('eci,eid->ecd', jax.nn.silu(G) * U, W_down)
            Yf = Y.reshape(EC, d) * slots_w[:, None]
            out = jnp.zeros((T, d), x.dtype).at[slots_token].add(Yf)
            shared = jax.nn.silu(x @ shared_gate.T) * (x @ shared_up.T) @ shared_down.T
            return (out + shared).reshape(b, s, d)
        key = jax.random.key(seed)
        ks = jax.random.split(key, 8)

        def rn(k, shape, scale=0.02):
            return jax.random.normal(k, shape, jnp.float32) * scale
        return {'hidden_states': jax.random.normal(ks[0], (B, S, D), jnp.float32), 'router_w': rn(ks[1], (E, D)), 'e_bias': jnp.zeros((E,), jnp.float32), 'W_gate': rn(ks[2], (E, D, I)), 'W_up': rn(ks[3], (E, D, I)), 'W_down': rn(ks[4], (E, I, D)), 'shared_gate': rn(ks[5], (I * NSH, D)), 'shared_up': rn(ks[6], (I * NSH, D)), 'shared_down': rn(ks[7], (D, I * NSH))}
    _L0_ffn_all = _L0_ffn_setup()
    _L0_ffn_in = {k: v for k, v in _L0_ffn_all.items() if k in ('router_w', 'e_bias', 'W_gate', 'W_up', 'W_down', 'shared_gate', 'shared_up', 'shared_down')}
    del _L0_ffn_all
    return {'x': x, 'ctx_2048': ctx_2048, 'mask_Bx1xS2_ff0': mask_Bx1xS2_ff0, 'L0_ffn_router_w': _L0_ffn_in['router_w'], 'L0_ffn_e_bias': _L0_ffn_in['e_bias'], 'L0_ffn_W_gate': _L0_ffn_in['W_gate'], 'L0_ffn_W_up': _L0_ffn_in['W_up'], 'L0_ffn_W_down': _L0_ffn_in['W_down'], 'L0_ffn_shared_gate': _L0_ffn_in['shared_gate'], 'L0_ffn_shared_up': _L0_ffn_in['shared_up'], 'L0_ffn_shared_down': _L0_ffn_in['shared_down']}

def reference(x, ctx_2048, mask_Bx1xS2_ff0, L0_ffn_router_w, L0_ffn_e_bias, L0_ffn_W_gate, L0_ffn_W_up, L0_ffn_W_down, L0_ffn_shared_gate, L0_ffn_shared_up, L0_ffn_shared_down):
    import jax
    import jax.numpy as jnp

    def _L0_xattn_ref(input, weight, bias):
        import jax, jax.numpy as jnp
        import numpy as np
        FP8_E4M3_MAX = 448.0
        EPS = 1e-12

        def _fp8_quant_dequant(x):
            amax = jnp.max(jnp.abs(x))
            scale = FP8_E4M3_MAX / jnp.maximum(amax, EPS)
            q = jnp.clip(x * scale, -FP8_E4M3_MAX, FP8_E4M3_MAX).astype(jnp.float8_e4m3fn)
            return q.astype(jnp.float32) / scale
        x_dq = _fp8_quant_dequant(input)
        w_dq = _fp8_quant_dequant(weight)
        out = jnp.einsum('bmk,bkn->bmn', x_dq, w_dq)
        out = out + bias
        return out

    def _L0_ffn_ref(hidden_states, router_w, e_bias, W_gate, W_up, W_down, shared_gate, shared_up, shared_down):
        import math
        import jax, jax.numpy as jnp
        import numpy as np
        from jax import lax
        D = 1024
        I = 512
        E = 32
        K = 4
        NG = 8
        TKG = 3
        NSH = 2
        SCALE = 2.5
        CF = 1.25
        B, S = (2, 1024)

        def _router(x, router_w, e_bias):
            scores = jax.nn.sigmoid(x @ router_w.T)
            sc = scores + e_bias[None, :]
            T = x.shape[0]
            gs = sc.reshape(T, NG, E // NG)
            group_scores = lax.top_k(gs, 2)[0].sum(-1)
            _, gidx = lax.top_k(group_scores, TKG)
            gmask = jnp.zeros((T, NG), sc.dtype).at[jnp.arange(T)[:, None], gidx].set(1.0)
            smask = jnp.repeat(gmask, E // NG, axis=1)
            masked = jnp.where(smask > 0, sc, 0.0)
            _, topk_idx = lax.top_k(masked, K)
            topk_w = jnp.take_along_axis(scores, topk_idx, axis=1)
            topk_w = topk_w / (topk_w.sum(-1, keepdims=True) + 1e-20)
            topk_w = topk_w * SCALE
            return (topk_idx.astype(jnp.int32), topk_w)

        def _moe_forward(hidden_states, router_w, e_bias, W_gate, W_up, W_down, shared_gate, shared_up, shared_down):
            b, s, d = hidden_states.shape
            T = b * s
            C = int(math.ceil(CF * T / E))
            EC = E * C
            x = hidden_states.reshape(T, d)
            topk_idx, topk_w = _router(x, router_w, e_bias)
            expert_flat = topk_idx.reshape(-1)
            w_flat = topk_w.reshape(-1)
            tok_flat = jnp.repeat(jnp.arange(T, dtype=jnp.int32), K)
            sort_ix = jnp.argsort(expert_flat)
            e_sorted = expert_flat[sort_ix]
            tok_s = tok_flat[sort_ix]
            w_s = w_flat[sort_ix]
            counts = jnp.zeros(E, jnp.int32).at[e_sorted].add(1)
            group_start = jnp.concatenate([jnp.zeros(1, jnp.int32), jnp.cumsum(counts)[:-1].astype(jnp.int32)])
            pos = jnp.arange(T * K, dtype=jnp.int32) - group_start[e_sorted]
            valid = pos < C
            dest = e_sorted * C + jnp.where(valid, pos, 0)
            slots_token = jnp.zeros(EC, jnp.int32).at[dest].add(jnp.where(valid, tok_s, 0))
            slots_w = jnp.zeros(EC, w_s.dtype).at[dest].add(jnp.where(valid, w_s, 0.0))
            Xp = x[slots_token].reshape(E, C, d)
            G = jnp.einsum('ecd,edi->eci', Xp, W_gate)
            U = jnp.einsum('ecd,edi->eci', Xp, W_up)
            Y = jnp.einsum('eci,eid->ecd', jax.nn.silu(G) * U, W_down)
            Yf = Y.reshape(EC, d) * slots_w[:, None]
            out = jnp.zeros((T, d), x.dtype).at[slots_token].add(Yf)
            shared = jax.nn.silu(x @ shared_gate.T) * (x @ shared_up.T) @ shared_down.T
            return (out + shared).reshape(b, s, d)
        return _moe_forward(hidden_states, router_w, e_bias, W_gate, W_up, W_down, shared_gate, shared_up, shared_down)
    x = x + _L0_xattn_ref(_layernorm(x, axis=-1), ctx_2048, mask_Bx1xS2_ff0)
    x = x + _L0_ffn_ref(_layernorm(x, axis=-1), L0_ffn_router_w, L0_ffn_e_bias, L0_ffn_W_gate, L0_ffn_W_up, L0_ffn_W_down, L0_ffn_shared_gate, L0_ffn_shared_up, L0_ffn_shared_down)
    return x

_drawn_inputs = setup_inputs


def setup_inputs(seed=0):
    import zlib

    import numpy as np

    out = dict(_drawn_inputs(seed))
    spreads = {'L0_ffn_e_bias': (0.0, 0.8)}
    factors = {'L0_ffn_router_w': 8.0,
     'L0_ffn_W_gate': 8.0,
     'L0_ffn_W_up': 8.0,
     'L0_ffn_W_down': 8.0,
     'L0_ffn_shared_gate': 8.0,
     'L0_ffn_shared_up': 8.0,
     'L0_ffn_shared_down': 8.0}
    for name, (base, spread) in spreads.items():
        noise = np.random.default_rng([zlib.crc32(name.encode()), seed]).standard_normal(out[name].shape)
        drawn = base * np.exp(spread * noise) if base else spread * noise
        out[name] = jnp.asarray(drawn.astype(out[name].dtype))
    for name, factor in factors.items():
        out[name] = (out[name] * factor).astype(out[name].dtype)
    return out
```

```python
from contextlib import ExitStack

import numpy as np

import concourse.bass as bass
from concourse import mybir

ALU = mybir.AluOpType
ACT = mybir.ActivationFunctionType
AX = mybir.AxisListType
F32 = mybir.dt.float32
F16 = mybir.dt.float16
BF16 = mybir.dt.bfloat16
I32 = mybir.dt.int32
U32 = mybir.dt.uint32

P = 128
LN_EPS = 1e-5
FP8_MAX = 448.0
EXPONENT_BITS = 0x7F800000
FP8_MIN_NORMAL = 2.0 ** -6
ROUNDER = 1.5 * 2.0 ** 20

X_SCALE = 2.0 ** 10
W_SCALE = 2.0 ** 4
H_SCALE = 2.0 ** -2
UP_PROJ = 1.0 / (X_SCALE * W_SCALE)
DOWN_PROJ = 1.0 / (H_SCALE * W_SCALE)
NO_SLOT = 1.0e6
ROUTED_SCALE = 2.5


def moe_kernel(nc, x, ctx_in, mask, router_t, e_bias, w_gate, w_up, w_down, sh_gate, sh_up, sh_down, out,
               xn_dram, slot_dram):
    T, D = x.shape
    E = router_t.shape[1]
    I = w_gate.shape[1]
    SI = sh_gate.shape[1]
    TOPK, NGRP, TOPG = 4, 8, 3
    EPG = E // NGRP
    C = -(-(5 * T) // (4 * E))
    HC = C // 2
    G = 256
    NT = G // P
    GROUPS = T // G
    KD = D // P
    KS = SI // P
    KI = I // P
    BATCH_TILES = 8
    HALF = 512
    CH = 4
    XCHUNKS = T // (CH * P)
    CCHUNKS = XCHUNKS - 2
    COLS = 2 * E

    with ExitStack() as stack:
        def sb(name, shape, dt):
            return stack.enter_context(nc.sbuf_tensor(name, shape, dt))

        def sem(name):
            return stack.enter_context(nc.semaphore(name))

        W = sb("W", [P, 49152], F16)
        BIG = sb("BIG", [P, 24576], BF16)
        X = sb("X", [P, 2 * NT * D], F32)
        FR = sb("FR", [P, 4096], F32)
        XT = sb("XT", [P, 2 * KD * G], F16)
        HH = sb("HH", [P, 2 * KS * G], F16)
        SG = sb("SG", [P, 5 * G], F32)

        identf = sb("identf", [P, P], F32)
        identb = sb("identb", [P, P], BF16)
        tri = sb("tri", [P, P], BF16)
        ones = sb("ones", [P, P], BF16)
        rw = sb("rw", [P, KD, 2 * E], F16)
        sel = sb("sel", [2 * E, E], F32)
        bias_sb = sb("bias_sb", [P, E], F32)
        lg = sb("lg", [2 * E, G], F32)
        iota_e = sb("iota_e", [P, E], F32)
        tokid = sb("tokid", [P, NT], F32)
        expo = sb("expo", [P, 4], F32)
        a1 = sb("a1", [P, T // P], F32)
        b1 = sb("b1", [P, T // P], F32)
        st1 = sb("st1", [P, CH, 2, 6], F32)
        mv1 = sb("mv1", [P, CH, 2], F32)
        ve1 = sb("ve1", [P, CH], F32)
        amax = sb("amax", [P, XCHUNKS + CCHUNKS + 4], F32)
        sc1 = sb("sc1", [P, 16], F32)
        st2 = sb("st2", [P, NT, 2, 6], F32)
        mv2 = sb("mv2", [P, NT, 2], F32)
        ve2 = sb("ve2", [P, NT], F32)
        rs2 = sb("rs2", [P, NT], F32)
        nb2 = sb("nb2", [P, NT], F32)
        s_sb = sb("s_sb", [P, NT, E], F32)
        sc = sb("sc", [P, NT, E], F32)
        masked = sb("masked", [P, NT, E], F32)
        g_a = sb("g_a", [P, NT * NGRP], F32)
        g_b = sb("g_b", [P, NT * NGRP], F32)
        g_c = sb("g_c", [P, NT * NGRP], F32)
        g_d = sb("g_d", [P, NT * NGRP], F32)
        g_top = sb("g_top", [P, NT, 8], F32)
        g_idx = sb("g_idx", [P, NT, 8], U32)
        g_idf = sb("g_idf", [P, NT, 8], F32)
        g_eq = sb("g_eq", [P, NT, TOPG, NGRP], F32)
        e_top = sb("e_top", [P, NT, 8], F32)
        e_idx = sb("e_idx", [P, NT, 8], U32)
        e_idf = sb("e_idf", [P, NT, TOPK], F32)
        e_eq = sb("e_eq", [P, NT, TOPK, E], F32)
        e_pr = sb("e_pr", [P, NT, TOPK, E], F32)
        r_w = sb("r_w", [P, NT, TOPK], F32)
        r_den = sb("r_den", [P, NT], F32)
        r_pos = sb("r_pos", [P, NT, TOPK], F32)
        r_ge = sb("r_ge", [P, NT, TOPK], F32)
        picks = sb("picks", [P, NT, E], BF16)
        cum = sb("cum", [P, E], F32)
        cumb = sb("cumb", [P, E], BF16)
        dest = sb("dest", [P, NT * TOPK], U32)
        payload = sb("payload", [P, NT * TOPK, 2], F32)
        tab = sb("tab", [HC, COLS, 2], F32)
        gidx = sb("gidx", [HC, COLS], U32)
        sidx = sb("sidx", [HC, COLS], U32)
        wts = sb("wts", [HC, COLS], F32)
        gix = sb("gix", [HC, 4], U32)
        six = sb("six", [HC, 4], U32)

        PS = [stack.enter_context(nc.psum_tensor(f"ps{i}", [P, 512], F32)) for i in range(8)]

        def wview(at, k, n):
            return W[:, at:at + k * n].rearrange("p (k n) -> p k n", k=k)

        SW = [[wview((2 * m + v) * 8192, 8, 1024) for v in range(2)] for m in range(3)]
        EW = [[[wview(b * 24576 + (2 * m + v) * 4096, KI if m == 2 else KD, D if m == 2 else I) for v in range(2)]
               for m in range(3)] for b in range(2)]
        p1_slot = [W[:, s * 8192:(s + 1) * 8192].bitcast(F32) for s in range(4)]
        sw_stage = [W[:, 32768 + 4096 * s:32768 + 4096 * (s + 1)].bitcast(F32) for s in range(4)]
        sd_stage = [BIG[:, 8192 + 4096 * s:8192 + 4096 * (s + 1)].bitcast(F32) for s in range(2)]
        ctx0 = [BIG[:, 8192 + 4096 * m:8192 + 4096 * (m + 1)].bitcast(F32) for m in range(4)]
        ctx_ring = [BIG[:, 16384 + 2048 * s:16384 + 2048 * (s + 1)].bitcast(F32) for s in range(2)]
        mask_sb = BIG[:, 20480:22528].bitcast(F32)
        M_main = BIG[:, 22528:24576].bitcast(F32)
        M_first = XT[:, 0:2048].bitcast(F32)
        ew_stage = [BIG[:, 4096 * m:4096 * (m + 1)].bitcast(F32) for m in range(6)]
        xbuf = [X[:, b * NT * D:(b + 1) * NT * D].rearrange("p (t d) -> p t d", t=NT) for b in range(2)]
        xn = [FR[:, j * D:(j + 1) * D] for j in range(NT)]
        xqT = FR[:, 2048:3072].bitcast(BF16).rearrange("p (k t) -> p k t", k=KD)
        xq = [FR[:, 3072 + 512 * j:3072 + 512 * (j + 1)].bitcast(BF16) for j in range(NT)]
        xT = [XT[:, v * KD * G:(v + 1) * KD * G].rearrange("p (k t) -> p k t", k=KD) for v in range(2)]
        hT = [HH[:, v * KS * G:(v + 1) * KS * G].rearrange("p (k t) -> p k t", k=KS) for v in range(2)]
        eT = [XT[:, v * KD * G:v * KD * G + KD * C].rearrange("p (k t) -> p k t", k=KD) for v in range(2)]
        ehT = [HH[:, v * KS * G:v * KS * G + KI * C].rearrange("p (k t) -> p k t", k=KI) for v in range(2)]
        sig = [SG[:, b * G:(b + 1) * G] for b in range(2)]
        h32 = [SG[:, (2 + b) * G:(3 + b) * G] for b in range(2)]
        gup = SG[:, 4 * G:5 * G]
        rw_f = SG[:, 0:KD * E].rearrange("p (k e) -> p k e", k=KD)
        zeros = HH[0:HC, :].bitcast(F32)
        slot_init = FR[0:E, 0:2 * C].rearrange("p (s w) -> p s w", s=C)
        ybuf = [X[0:HC, b * 2048:(b + 1) * 2048].rearrange("p (t d) -> p t d", t=2) for b in range(2)]
        xg = [FR[0:HC, b * 2048:(b + 1) * 2048].rearrange("p (t d) -> p t d", t=2) for b in range(2)]
        logit_ps = PS[2][0:2 * E, 0:G]
        score_ps = PS[3][:, 0:NT * E]
        pos_ps = PS[3][:, 64:64 + NT * E].rearrange("p (t e) -> p t e", t=NT)

        ld_small = sem("ld_small")
        ld_p1 = [sem(f"ld_p1_{s}") for s in range(4)]
        ld_c0 = [sem(f"ld_c0_{m}") for m in range(4)]
        ld_sw = [sem(f"ld_sw{s}") for s in range(6)]
        ld_x = [sem(f"ld_x{b}") for b in range(2)]
        ld_mask = sem("ld_mask")
        ld_ctx = [sem(f"ld_ctx{b}") for b in range(2)]
        ld_tab = sem("ld_tab")
        ld_ew = [sem(f"ld_ew{m}") for m in range(6)]
        ld_xg = [sem(f"ld_xg{b}") for b in range(2)]
        st_init = sem("st_init")
        st_xn = [sem(f"st_xn{j}") for j in range(NT)]
        st_out = [sem(f"st_out{b}") for b in range(2)]
        st_slot = sem("st_slot")
        st_y = [sem(f"st_y{b}") for b in range(2)]
        consts_ready = sem("consts_ready")
        pool_step = sem("pool_step")
        ve1_ready, rs1_ready, nb1_ready, ln1_done, p1_done = map(sem, ("ve1_ready", "rs1_ready", "nb1_ready", "ln1_done", "p1_done"))
        amax_ready, amax_all, scales_ready = map(sem, ("amax_ready", "amax_all", "scales_ready"))
        sw_hi, sw_lo, rw_hi, rw_lo = map(sem, ("sw_hi", "sw_lo", "rw_hi", "rw_lo"))
        pe_gu, pe_xq, pe_xa, pe_xt, pe_dn, pe_lg, pe_lt, pe_pos = map(
            sem, ("pe_gu", "pe_xq", "pe_xa", "pe_xt", "pe_dn", "pe_lg", "pe_lt", "pe_pos"))
        a_v, a_cv, a_xq, a_xn, a_xh, a_sig, a_hh, a_lg, a_sc = map(
            sem, ("a_v", "a_cv", "a_xq", "a_xn", "a_xh", "a_sig", "a_hh", "a_lg", "a_sc"))
        d_q, d_cq, d_x2, d_var, d_nb, d_xl, d_t, d_h, d_hl, d_out, d_picks, d_route, d_chain = map(
            sem, ("d_q", "d_cq", "d_x2", "d_var", "d_nb", "d_xl", "d_t", "d_h", "d_hl", "d_out", "d_picks",
                  "d_route", "d_chain"))
        p_xm, p_rs, p_carry = map(sem, ("p_xm", "p_rs", "p_carry"))
        x_gu, x_xt, x_dn, x_hi, x_lo, x_sig, x_hh, x_xh, x_y, x_t, x_h, x_hl, x_xl = map(
            sem, ("x_gu", "x_xt", "x_dn", "x_hi", "x_lo", "x_sig", "x_hh", "x_xh", "x_y", "x_t", "x_h", "x_hl", "x_xl"))

        def wait(eng, s, value):
            if isinstance(value, int) and value <= 0:
                return
            eng.wait_ge(s, value)

        def settle(eng):
            eng.wait_ge(consts_ready, 2)

        def carry(engine, col):
            return engine.tensor_tensor(expo[:, col:col + 1], expo[:, 0:1], expo[:, 0:1], ALU.add)

        class Chain:

            def __init__(self, eng, s):
                self.eng, self.s, self.before, self.n = eng, s, 0, 0

            def do(self, ins):
                ins.then_inc(self.s, 1)
                self.n += 1

            def sync(self):
                self.eng.wait_ge(self.s, self.before + self.n)

            def link(self, ins):
                self.do(ins)
                self.sync()

            def close(self):
                self.before, self.n = self.before + self.n, 0

        SW_PIECES = [(m, kh, ih) for ih in range(2) for m in range(2) for kh in range(2)]
        SW_PIECES += [(2, kh, nh) for nh in range(2) for kh in range(2)]
        sw_dram = [sh_gate, sh_up, sh_down]

        def sw_slot(n):
            return (n % 4, sw_stage[n % 4]) if n < 8 else (4 + n % 2, sd_stage[n % 2])

        def sw_uses(n):
            return n // 4 + 1 if n < 8 else (n - 8) // 2 + 1

        def rows(dram, start, count):
            return dram[bass.ds(start, count), :]

        block = stack.enter_context(nc.Block())

        @block.sync
        def _(sp):
            sp.dma_start(rw_f, router_t.rearrange("(k p) e -> p k e", p=P)).then_inc(ld_small, 16)
            sp.dma_start(bias_sb[:, :], e_bias.partition_broadcast(P)).then_inc(ld_small, 16)

            def p1_load(c):
                wait(sp, p1_done, c - 3)
                src, r = (x, c * CH * P) if c < XCHUNKS else (ctx_in, (c - XCHUNKS + 2) * CH * P)
                sp.dma_start(p1_slot[c % 4].rearrange("p (t d) -> p t d", t=CH),
                             src[r:r + CH * P, :].rearrange("(t p) d -> p t d", p=P)).then_inc(ld_p1[c % 4], 16)

            def sw_load(n):
                s, stage = sw_slot(n)
                if n < 8:
                    wait(sp, sw_lo, n - 3)
                elif n < 10:
                    wait(sp, d_cq, 2 * (n - 8) + 2)
                else:
                    wait(sp, sw_lo, n - 1)
                m, kh, ih = SW_PIECES[n]
                sp.dma_start(stage.rearrange("p (k i) -> p k i", k=4),
                             sw_dram[m][kh * 512:(kh + 1) * 512, ih * 512:(ih + 1) * 512]
                             .rearrange("(k p) i -> p k i", p=P)).then_inc(ld_sw[s], 16)

            def x_load(f, b):
                sp.dma_start(xbuf[b], rows(x, f * G, G).rearrange("(t p) d -> p t d", p=P)).then_inc(ld_x[b], 16)

            def mask_load(f):
                sp.dma_start(mask_sb, rows(mask, f >> 2, 1).squeeze(0).partition_broadcast(P)).then_inc(ld_mask, 16)

            for c in range(XCHUNKS):
                p1_load(c)
                if c == 3:
                    sp.wait_ge(consts_ready, 2)
                    sp.dma_start(out[T:T + C, :].rearrange("(t p) d -> p t d", p=HC),
                                 zeros.rearrange("p (t d) -> p t d", t=2)).then_inc(st_init, 16)
                    sp.dma_start(slot_dram.rearrange("(e s) w -> e s w", e=E), slot_init).then_inc(st_init, 16)

            x_load(0, 0)
            for c in range(XCHUNKS, XCHUNKS + CCHUNKS):
                p1_load(c)
            for m in range(4):
                sp.dma_start(ctx0[m].rearrange("p (t d) -> p t d", t=2),
                             ctx_in[m * 256:(m + 1) * 256, :].rearrange("(t p) d -> p t d", p=P)).then_inc(ld_c0[m], 16)
            for n in range(4):
                sw_load(n)
            sp.wait_ge(d_cq, 8)
            mask_load(0)
            for n in range(4, 12):
                sw_load(n)

            def xn_stores(f):
                for j in range(NT):
                    wait(sp, a_xn, 2 * f + j + 1)
                    sp.dma_start(rows(xn_dram, f * G + j * P, P), xn[j]).then_inc(st_xn[j], 16)

            def group(g, r, front=True, ctx_piece=True):
                if front:
                    wait(sp, st_out[1 - r], (g + r) * 16)
                    x_load(g + 1, 1 - r)
                    wait(sp, p_xm, 2 * g + 2)
                    mask_load(g + 1)
                if ctx_piece:
                    for j in range(2):
                        wait(sp, d_cq, 2 * g + 8 - 1 + j)
                        sp.dma_start(ctx_ring[j], rows(ctx_in, (2 * g + 8 + j) * P, P)).then_inc(ld_ctx[j], 16)
                if front:
                    xn_stores(g + 1)
                for j in range(NT):
                    wait(sp, d_out, 4 * g + 2 * j + 2)
                    sp.dma_start(rows(out, g * G + j * P, P), xbuf[r][:, j, :]).then_inc(st_out[r], 16)

            xn_stores(0)
            group(0, 0)
            group(1, 1)
            with sp.Fori(1, 6) as pair:
                group(pair * 2, 0)
                group(pair * 2 + 1, 1)
            for g in range(12, GROUPS - 1):
                group(g, g % 2, ctx_piece=False)

            def ew_load(e, m):
                if m < 4:
                    src = rows((w_gate, w_up)[m // 2], e * D + (m % 2) * 512, 512)
                    dst = ew_stage[m].rearrange("p (k i) -> p k i", k=4)
                else:
                    src = rows(w_down, e * I + (m % 2) * 256, 256)
                    dst = ew_stage[m].rearrange("p (k i) -> p k i", k=2)
                sp.dma_start(dst, src.rearrange("(k p) i -> p k i", p=P)).then_inc(ld_ew[m], 16)

            sp.wait_ge(pe_xa, 4 * GROUPS)
            sp.wait_ge(p_xm, 2 * GROUPS)
            for m in range(6):
                ew_load(0, m)
            sp.wait_ge(st_slot, 16 * NT * TOPK * GROUPS)
            with nc.allow_non_contiguous_dma(reason="the slot table is read once"):
                sp.dma_start(tab[:, :, :], slot_dram.rearrange("(c p) w -> p c w", p=HC)).then_inc(ld_tab, 16)
            group(GROUPS - 1, 1, front=False, ctx_piece=False)
            with sp.Fori(1, E) as e:
                for m in range(6):
                    wait(sp, x_lo, e * 6 + (m - 5))
                    ew_load(e, m)
            sp.wait_ge(st_y[0], 16 * E)
            sp.wait_ge(st_y[1], 16 * E)

        @block.gpsimd
        def _(pool):
            gp = nc.gpsimd
            ch = Chain(pool, pool_step)
            ch.do(gp.memset(zeros, 0.0))
            ch.do(gp.iota(slot_init[:, :, 0], [[1, C]], base=T, channel_multiplier=0,
                          allow_small_or_imprecise_dtypes=True))
            ch.do(gp.memset(slot_init[:, :, 1], 0.0))
            ch.do(gp.memset(identf[:, :], 0.0))
            ch.do(gp.memset(tri[:, :], 1.0))
            ch.do(gp.memset(ones[:, :], 1.0))
            ch.do(gp.memset(sel[:, :], 0.0))
            ch.do(gp.memset(expo[:, :], -0.5))
            ch.do(gp.memset(cum[:, :], 0.0))
            ch.do(gp.memset(cumb[:, :], 0.0))
            ch.do(gp.iota(iota_e[:, :], [[1, E]], base=0, channel_multiplier=0, allow_small_or_imprecise_dtypes=True))
            ch.do(gp.iota(tokid[:, :], [[P, NT]], base=0, channel_multiplier=1, allow_small_or_imprecise_dtypes=True))
            ch.sync()
            ch.do(gp.affine_select(out=identf[:, :], in_=identf[:, :], compare_op=ALU.not_equal, fill=1.0, base=0,
                                   pattern=[[-1, P]], channel_multiplier=1))
            ch.do(gp.affine_select(out=tri[:, :], in_=tri[:, :], compare_op=ALU.is_gt, fill=0.0, base=0,
                                   pattern=[[1, P]], channel_multiplier=-1))
            for half in range(2):
                ch.link(gp.affine_select(out=sel[:, :], in_=sel[:, :], compare_op=ALU.not_equal, fill=1.0,
                                         base=-E * half, pattern=[[-1, E]], channel_multiplier=1))
            gp.tensor_copy(identb[:, :], identf[:, :]).then_inc(consts_ready, 2)

            for c in range(XCHUNKS):
                pool.wait_ge(ve1_ready, c + 1)
                gp.tensor_tensor(a1[:, c * CH:(c + 1) * CH], ve1[:, :], expo[:, 0:CH], ALU.pow).then_inc(rs1_ready, 1)
            for n in range(2):
                pool.wait_ge(amax_ready, n + 1)
                gp.partition_all_reduce(sc1[:, 4 * n + 1:4 * n + 2], sc1[:, 4 * n:4 * n + 1], P,
                                        bass.bass_isa.ReduceOp.max).then_inc(amax_all, 1)

            def pool_carry(before):
                wait(pool, p_carry, before)
                carry(gp, 2).then_inc(p_carry, 1)

            def add_mask(f, b):
                pool.wait_ge(ld_mask, 16 * f + 16)
                for j in range(NT):
                    pool.wait_ge(a_v, 2 * f + j + 1)
                    gp.tensor_tensor(xbuf[b][:, j, :], xbuf[b][:, j, :], mask_sb, ALU.add).then_inc(p_xm, 1)

            def rstd2(f):
                wait(pool, a_xn, 2 * f)
                for j in range(NT):
                    pool.wait_ge(d_var, 2 * f + j + 1)
                    gp.tensor_tensor(rs2[:, j:j + 1], ve2[:, j:j + 1], expo[:, 0:1], ALU.pow).then_inc(p_rs, 1)

            def fill_slots(g):
                pool.wait_ge(d_route, g + 1)
                pool_carry(g)
                for m in range(NT * TOPK):
                    gp.indirect_dma_start(out=slot_dram[:, :],
                                          out_offset=bass.IndirectOffsetOnAxis(ap=dest[:, m:m + 1], axis=0),
                                          in_=payload[:, m, :], in_offset=None,
                                          bounds_check=E * C - 1, oob_is_err=False).then_inc(st_slot, 16)

            add_mask(0, 0)
            rstd2(0)
            pool.wait_ge(st_init, 32)

            def group(g, r, front=True):
                if front:
                    add_mask(g + 1, 1 - r)
                    rstd2(g + 1)
                fill_slots(g)

            group(0, 0)
            group(1, 1)
            with pool.Fori(1, 6) as pair:
                group(pair * 2, 0)
                group(pair * 2 + 1, 1)
            for g in range(12, GROUPS):
                group(g, g % 2, front=g < GROUPS - 1)

            pool.wait_ge(ld_tab, 16)
            ch.do(gp.tensor_scalar(gidx[:, :], tab[:, :, 0], float(T - 1), None, ALU.min))
            ch.do(gp.tensor_copy(sidx[:, :], tab[:, :, 0]))
            ch.do(gp.tensor_scalar(wts[:, :], tab[:, :, 1], DOWN_PROJ, None, ALU.mult))
            ch.sync()
            ch.close()
            SLOT_STEPS = ch.before

            def cols(e):
                return bass.ds(e * 2, 2)

            def gather(e, b, step, carries):
                gp.tensor_copy(gix[:, 2 * b:2 * b + 2], gidx[:, cols(e)]).then_inc(pool_step, 1)
                pool.wait_ge(pool_step, step)
                pool_carry(carries)
                for blk in range(2):
                    gp.indirect_dma_start(out=xg[b][:, blk, :], out_offset=None, in_=xn_dram[:, :],
                                          in_offset=bass.IndirectOffsetOnAxis(ap=gix[:, 2 * b + blk:2 * b + blk + 1],
                                                                              axis=0),
                                          bounds_check=T - 1, oob_is_err=False).then_inc(ld_xg[b], 16)

            def scatter(e, b, step, carries):
                gp.tensor_copy(six[:, 2 * b:2 * b + 2], sidx[:, cols(e)]).then_inc(pool_step, 1)
                pool.wait_ge(pool_step, step)
                pool.wait_ge(x_y, e * 4 + 4)
                pool_carry(carries)
                for blk in range(2):
                    gp.indirect_dma_start(out=out[:, :],
                                          out_offset=bass.IndirectOffsetOnAxis(ap=six[:, 2 * b + blk:2 * b + blk + 1],
                                                                               axis=0),
                                          in_=ybuf[b][:, blk, :], in_offset=None, bounds_check=T + C - 1,
                                          oob_is_err=True, compute_op=ALU.add).then_inc(st_y[b], 16)

            for j in range(NT):
                pool.wait_ge(st_xn[j], 16 * GROUPS)
            pool.wait_ge(pe_xt, 4 * GROUPS)
            gather(0, 0, SLOT_STEPS + 1, GROUPS)
            gather(1, 1, SLOT_STEPS + 2, GROUPS + 1)
            for b in range(2):
                pool.wait_ge(st_out[b], 16 * GROUPS)

            def expert(e, b, more=True):
                steps = e * 2 + (SLOT_STEPS + 3)
                if b == 1:
                    pool.wait_ge(st_y[0], e * 16 + 16)
                else:
                    wait(pool, st_y[1], e * 16)
                carries = e * 4 + (GROUPS + 2)
                if not more:
                    steps = SLOT_STEPS + 2 * E + (e - (E - 2)) - 1
                    carries = 4 * (E - 2) + GROUPS + 2 + 2 * (e - (E - 2))
                pool_carry(carries)
                scatter(e, b, steps, carries + 1)
                if more:
                    pool.wait_ge(x_xt, e * 3 + 3)
                    pool_carry(carries + 2)
                    gather(e + 2, b, steps + 1, carries + 3)

            expert(0, 0)
            expert(1, 1)
            with pool.Fori(1, E // 2 - 1) as pair:
                expert(pair * 2, 0)
                expert(pair * 2 + 1, 1)
            expert(E - 2, 0, more=False)
            expert(E - 1, 1, more=False)
            for b in range(2):
                pool.wait_ge(st_y[b], 16 * E)

        @block.scalar
        def _(act):
            ac = nc.scalar

            def split_hi(n):
                s, stage = sw_slot(n)
                act.wait_ge(ld_sw[s], 16 * sw_uses(n))
                if n == 0:
                    act.wait_ge(p1_done, XCHUNKS + CCHUNKS)
                if n == 8:
                    act.wait_ge(sw_lo, 8)
                m, kh, ih = SW_PIECES[n]
                ac.activation(SW[m][0][:, kh * 4:kh * 4 + 4, ih * 512:(ih + 1) * 512],
                              stage.rearrange("p (k i) -> p k i", k=4), ACT.Copy, scale=W_SCALE).then_inc(sw_hi, 1)

            act.wait_ge(ld_small, 32)
            ac.activation(rw[:, :, 0:E], rw_f, ACT.Copy, scale=W_SCALE).then_inc(rw_hi, 1)

            for c in range(XCHUNKS):
                act.wait_ge(nb1_ready, c + 1)
                for t in range(CH):
                    at = p1_slot[c % 4][:, t * D:(t + 1) * D]
                    n = c * CH + t
                    ins = ac.activation(at, at, ACT.Identity, bias=b1[:, n:n + 1], scale=a1[:, n:n + 1])
                ins.then_inc(ln1_done, 1)

            def x_scaled(f, b):
                settle(act)
                act.wait_ge(ld_x[b], 16 * (f // 2 + 1) if isinstance(f, int) else (f - b) * 8 + 16)
                for j in range(NT):
                    settle(act)
                    wait(act, st_xn[j], 16 * f)
                    wait(act, pe_xt, 4 * f)
                    n = 2 * f + j
                    ac.activation(xn[j], xbuf[b][:, j, :], ACT.Identity, bias=b1[:, bass.ds(n, 1)],
                                  scale=a1[:, bass.ds(n, 1)]).then_inc(a_v, 1)

            def ctx_scaled(view):
                ac.activation(view, view, ACT.Copy, scale=sc1[:, 6:7]).then_inc(a_cv, 1)

            def xq_evac(f):
                wait(act, pe_xa, 4 * f)
                for j in range(NT):
                    act.wait_ge(pe_xq, 2 * f + j + 1)
                    ac.activation(xqT[:, :, j * P:(j + 1) * P],
                                  PS[6 + j][:, :].bitcast(BF16).rearrange("p (k t) -> p k t", k=KD),
                                  ACT.Copy).then_inc(a_xq, 1)

            def ln2(f, b):
                for j in range(NT):
                    act.wait_ge(d_nb, 2 * f + j + 1)
                    ac.activation(xn[j], xbuf[b][:, j, :], ACT.Identity, bias=nb2[:, j:j + 1],
                                  scale=rs2[:, j:j + 1]).then_inc(a_xn, 1)

            def xt_hi(f):
                for j in range(NT):
                    for h in range(2):
                        act.wait_ge(pe_xt, 4 * f + 2 * j + h + 1)
                        ac.activation(xT[0][:, 4 * h:4 * h + 4, j * P:(j + 1) * P],
                                      PS[6 + h][:, :].rearrange("p (k t) -> p k t", k=4), ACT.Copy,
                                      scale=X_SCALE).then_inc(a_xh, 1)

            act.wait_ge(scales_ready, 1)
            act.wait_ge(st_init, 32)
            x_scaled(0, 0)
            xq_evac(0)
            act.wait_ge(scales_ready, 2)
            for m in range(4):
                for j in range(2):
                    ctx_scaled(ctx0[m][:, j * D:(j + 1) * D])
            for n in range(4):
                split_hi(n)
            ln2(0, 0)
            for n in range(4, 8):
                split_hi(n)
            xt_hi(0)
            for n in range(8, 12):
                split_hi(n)

            def group(g, r, front=True, ctx_piece=True, weights=None):
                for ic in range(KS):
                    act.wait_ge(pe_gu, 8 * g + ic + 1)
                    wait(act, d_t, 8 * g + (ic - 1 if ic > 1 else 0))
                    ac.activation(sig[ic % 2], PS[ic % 2][:, 0:G], ACT.Sigmoid, scale=UP_PROJ).then_inc(a_sig, 1)
                    act.wait_ge(d_h, 8 * g + ic + 1)
                    if ic == 0:
                        wait(act, pe_dn, 4 * g)
                    ac.activation(hT[0][:, ic, :], h32[ic % 2], ACT.Copy).then_inc(a_hh, 1)
                    if ic == 0:
                        act.wait_ge(pe_lg, g + 1)
                        ac.activation(lg[:, :], logit_ps, ACT.Copy, scale=UP_PROJ).then_inc(a_lg, 1)
                    if ic == 1:
                        act.wait_ge(pe_lt, g + 1)
                        wait(act, d_route, g)
                        ac.activation(s_sb[:, :, :], score_ps.rearrange("p (t e) -> p t e", t=NT),
                                      ACT.Sigmoid).then_inc(a_sc, 1)
                        if front:
                            x_scaled(g + 1, 1 - r)
                    if ctx_piece and ic in (3, 4):
                        j = ic - 3
                        act.wait_ge(ld_ctx[j], 16 * g + 16)
                        ctx_scaled(ctx_ring[j])
                    if front and ic == 6:
                        xq_evac(g + 1)
                if weights:
                    weights()
                if front:
                    ln2(g + 1, 1 - r)
                    xt_hi(g + 1)

            act.wait_ge(rw_lo, 1)
            group(0, 0)
            group(1, 1)
            with act.Fori(1, 6) as pair:
                group(pair * 2, 0)
                group(pair * 2 + 1, 1)
            for g in range(12, GROUPS - 1):
                group(g, g % 2, ctx_piece=False)

            def ew_hi(e, b, m, first=False):
                act.wait_ge(ld_ew[m], e * 16 + 16)
                if first and m == 0:
                    act.wait_ge(pe_gu, 8 * GROUPS)
                if not first:
                    wait(act, x_gu if m < 4 else x_dn, e * 4 - 4)
                stage = ew_stage[m]
                if m < 4:
                    dst = EW[b][m // 2][0][:, (m % 2) * 4:(m % 2) * 4 + 4, :]
                    stage = stage.rearrange("p (k i) -> p k i", k=4)
                else:
                    dst = EW[b][2][0][:, (m % 2) * 2:(m % 2) * 2 + 2, :]
                    stage = stage.rearrange("p (k i) -> p k i", k=2)
                ac.activation(dst, stage, ACT.Copy, scale=W_SCALE).then_inc(x_hi, 1)

            def et_hi(e):
                for s in range(3):
                    k = 3 if s < 2 else 2
                    act.wait_ge(x_xt, e * 3 + (s + 1))
                    ac.activation(eT[0][:, 3 * s:3 * s + k, :],
                                  PS[(2, 3, 6)[s]][:, 0:k * C].rearrange("p (k t) -> p k t", k=k), ACT.Copy,
                                  scale=X_SCALE).then_inc(x_xh, 1)

            group(GROUPS - 1, 1, front=False, ctx_piece=False,
                  weights=lambda: [ew_hi(0, 0, m, first=True) for m in range(6)])
            et_hi(0)
            act.wait_ge(pe_dn, 4 * GROUPS)
            for b in range(2):
                act.wait_ge(st_out[b], 16 * GROUPS)

            def expert(e, b, more=True):
                for ic in range(KI):
                    act.wait_ge(x_gu, e * 4 + (ic + 1))
                    wait(act, x_t, e * 4 + (ic - 1 if ic > 1 else 0))
                    ac.activation(sig[ic % 2][:, 0:C], PS[ic % 2][:, 0:C], ACT.Sigmoid, scale=UP_PROJ).then_inc(x_sig, 1)
                    act.wait_ge(x_h, e * 4 + (ic + 1))
                    if ic == 0:
                        wait(act, x_dn, e * 4)
                    ac.activation(ehT[0][:, ic, :], h32[ic % 2][:, 0:C], ACT.Copy).then_inc(x_hh, 1)
                    if more and ic < 3:
                        ew_hi(e + 1, 1 - b, ic)
                if more:
                    et_hi(e + 1)
                for u in range(4):
                    blk, hf = u // 2, u % 2
                    if more and u != 2:
                        ew_hi(e + 1, 1 - b, (3, 4, None, 5)[u])
                    settle(act)
                    if u == 0:
                        wait(act, st_y[b], (e - b) * 16)
                    act.wait_ge(x_dn, e * 4 + (u + 1))
                    ac.activation(ybuf[b][:, blk, hf * HALF:(hf + 1) * HALF], PS[4 + u % 2][0:HC, :], ACT.Copy,
                                  scale=wts[:, bass.ds(e * 2 + blk, 1)]).then_inc(x_y, 1)

            expert(0, 0)
            expert(1, 1)
            with act.Fori(1, E // 2 - 1) as pair:
                expert(pair * 2, 0)
                expert(pair * 2 + 1, 1)
            expert(E - 2, 0)
            expert(E - 1, 1, more=False)

        @block.vector
        def _(dve):
            ve = nc.vector
            ch = Chain(dve, d_chain)

            dve.wait_ge(consts_ready, 2)
            dve.wait_ge(rw_hi, 1)
            ve.scalar_tensor_tensor(out=rw[:, :, E:2 * E], in0=rw_f, scalar=W_SCALE, in1=rw[:, :, 0:E],
                                    op0=ALU.mult, op1=ALU.subtract).then_inc(rw_lo, 1)

            def abs_max(view, col):
                ins = ve.tensor_reduce(amax[:, col:col + 1], view, AX.X, ALU.max, apply_absolute_value=True)
                return ins

            def x_abs_max(c):
                dve.wait_ge(ln1_done, c + 1)
                abs_max(p1_slot[c % 4], c).then_inc(p1_done, 1)

            for c in range(XCHUNKS):
                dve.wait_ge(ld_p1[c % 4], 16 * (c // 4 + 1))
                for t in range(CH):
                    for h in range(2):
                        ch.do(ve.bn_stats(st1[:, t, h, :], p1_slot[c % 4][:, t * D + h * HALF:t * D + (h + 1) * HALF]))
                ch.sync()
                for t in range(CH):
                    ch.do(ve.bn_aggr(mv1[:, t, :], st1[:, t, :, :]))
                ch.sync()
                ve.tensor_scalar(ve1[:, :], mv1[:, :, 1], LN_EPS, None, ALU.add).then_inc(ve1_ready, 1)
                if c:
                    x_abs_max(c - 1)
                dve.wait_ge(rs1_ready, c + 1)
                ve.scalar_tensor_tensor(out=b1[:, c * CH:(c + 1) * CH], in0=mv1[:, :, 0], scalar=-1.0,
                                        in1=a1[:, c * CH:(c + 1) * CH], op0=ALU.mult, op1=ALU.mult).then_inc(nb1_ready, 1)
            x_abs_max(XCHUNKS - 1)
            dve.wait_ge(p1_done, XCHUNKS)
            ve.tensor_reduce(sc1[:, 0:1], amax[:, 0:XCHUNKS], AX.X, ALU.max).then_inc(amax_ready, 1)

            def ctx_abs_max(c):
                dve.wait_ge(ld_p1[c % 4], 16 * (c // 4 + 1))
                abs_max(p1_slot[c % 4], c).then_inc(p1_done, 1)

            def fp8_scale(n):
                at = 4 * n
                dve.wait_ge(amax_all, n + 1)
                ch.link(ve.tensor_scalar(sc1[:, at + 1:at + 2], sc1[:, at + 1:at + 2], 1e-12, None, ALU.max))
                ch.link(ve.reciprocal(sc1[:, at + 3:at + 4], sc1[:, at + 1:at + 2]))
                ch.link(ve.tensor_scalar(sc1[:, at + 2:at + 3], sc1[:, at + 3:at + 4], FP8_MAX, None, ALU.mult))
                ch.link(ve.reciprocal(sc1[:, at + 3:at + 4], sc1[:, at + 2:at + 3]))

            def fp8_round(v, scratch, dst):
                ch.link(ve.tensor_scalar(v, v, FP8_MAX, -FP8_MAX, ALU.min, ALU.max))
                ch.link(ve.tensor_scalar(scratch.bitcast(I32), v.bitcast(I32), EXPONENT_BITS, None, ALU.bitwise_and))
                ch.link(ve.tensor_scalar(scratch, scratch, FP8_MIN_NORMAL, ROUNDER, ALU.max, ALU.mult))
                ch.link(ve.tensor_tensor(v, v, scratch, ALU.add))
                return ve.tensor_tensor(dst, v, scratch, ALU.subtract)

            def x_round(f, j, scratch):
                dve.wait_ge(a_v, 2 * f + j + 1)
                wait(dve, pe_xq, 2 * f)
                fp8_round(xn[j], scratch, xq[j]).then_inc(d_q, 1)

            ctx_abs_max(XCHUNKS)
            fp8_scale(0)
            ch.do(ve.tensor_scalar(a1[:, :], a1[:, :], sc1[:, 2:3], None, ALU.mult))
            ch.do(ve.tensor_scalar(b1[:, :], b1[:, :], sc1[:, 2:3], None, ALU.mult))
            ch.sync()
            ve.tensor_copy(sc1[:, 8:9], sc1[:, 2:3]).then_inc(scales_ready, 1)
            ctx_abs_max(XCHUNKS + 1)
            for j in range(NT):
                x_round(0, j, M_first)
            for c in range(XCHUNKS + 2, XCHUNKS + CCHUNKS):
                ctx_abs_max(c)
            for m in range(4):
                dve.wait_ge(ld_c0[m], 16)
                ch.do(abs_max(ctx0[m], XCHUNKS + CCHUNKS + m))
            ch.sync()
            dve.wait_ge(p1_done, XCHUNKS + CCHUNKS)
            ve.tensor_reduce(sc1[:, 4:5], amax[:, XCHUNKS:], AX.X, ALU.max).then_inc(amax_ready, 1)
            fp8_scale(1)
            ve.tensor_tensor(sc1[:, 9:10], sc1[:, 3:4], sc1[:, 7:8], ALU.mult).then_inc(scales_ready, 1)

            dve.wait_ge(scales_ready, 2)
            for m in range(4):
                for j in range(2):
                    dve.wait_ge(a_cv, 2 * m + j + 1)
                    n = 2 * m + j
                    fp8_round(ctx0[m][:, j * D:(j + 1) * D], M_first, BIG[:, n * D:(n + 1) * D]).then_inc(d_cq, 1)

            def split_lo(n):
                s, stage = sw_slot(n)
                m, kh, ih = SW_PIECES[n]
                dve.wait_ge(sw_hi, n + 1)
                cut = (slice(None), slice(kh * 4, kh * 4 + 4), slice(ih * 512, (ih + 1) * 512))
                ve.scalar_tensor_tensor(out=SW[m][1][cut], in0=stage.rearrange("p (k i) -> p k i", k=4),
                                        scalar=W_SCALE, in1=SW[m][0][cut], op0=ALU.mult,
                                        op1=ALU.subtract).then_inc(sw_lo, 1)

            def residual(f, b):
                for j in range(NT):
                    dve.wait_ge(p_xm, 2 * f + j + 1)
                    for h in range(2):
                        at = xbuf[b][:, j, h * HALF:(h + 1) * HALF]
                        dve.wait_ge(pe_xa, 4 * f + 2 * j + h + 1)
                        ve.scalar_tensor_tensor(out=at, in0=PS[2 + h][:, :], scalar=sc1[:, 9:10], in1=at,
                                                op0=ALU.mult, op1=ALU.add).then_inc(d_x2, 1)
                    dve.wait_ge(d_x2, 4 * f + 2 * j + 2)
                    for h in range(2):
                        ch.do(ve.bn_stats(st2[:, j, h, :], xbuf[b][:, j, h * HALF:(h + 1) * HALF]))
                    ch.sync()
                    carry(ve, 1)
                    ch.link(ve.bn_aggr(mv2[:, j, :], st2[:, j, :, :]))
                    ve.tensor_scalar(ve2[:, j:j + 1], mv2[:, j, 1:2], LN_EPS, None, ALU.add).then_inc(d_var, 1)

            def shift(f):
                for j in range(NT):
                    dve.wait_ge(p_rs, 2 * f + j + 1)
                    ve.scalar_tensor_tensor(out=nb2[:, j:j + 1], in0=mv2[:, j, 0:1], scalar=-1.0, in1=rs2[:, j:j + 1],
                                            op0=ALU.mult, op1=ALU.mult).then_inc(d_nb, 1)

            def xt_lo(f, j):
                for h in range(2):
                    dve.wait_ge(a_xh, 4 * f + 2 * j + h + 1)
                    ve.scalar_tensor_tensor(out=xT[1][:, 4 * h:4 * h + 4, j * P:(j + 1) * P],
                                            in0=PS[6 + h][:, :].rearrange("p (k t) -> p k t", k=4), scalar=X_SCALE,
                                            in1=xT[0][:, 4 * h:4 * h + 4, j * P:(j + 1) * P],
                                            op0=ALU.mult, op1=ALU.subtract).then_inc(d_xl, 1)

            for n in range(2):
                split_lo(n)
            residual(0, 0)
            for n in range(2, 4):
                split_lo(n)
            shift(0)
            for n in range(4, 8):
                split_lo(n)
            xt_lo(0, 0)
            xt_lo(0, 1)
            for n in range(8, 12):
                split_lo(n)

            def route_picks(g):
                dve.wait_ge(a_sc, g + 1)
                ch.link(ve.tensor_tensor(sc[:, :, :], s_sb[:, :, :], bias_sb[:, :].unsqueeze(1).to_broadcast([P, NT, E]),
                                         ALU.add))
                q = sc[:, :, :].rearrange("p t (g i) -> p (t g) i", i=EPG)
                ch.do(ve.tensor_tensor(g_a[:, :], q[:, :, 0], q[:, :, 1], ALU.max))
                ch.do(ve.tensor_tensor(g_b[:, :], q[:, :, 2], q[:, :, 3], ALU.max))
                ch.do(ve.tensor_tensor(g_c[:, :], q[:, :, 0], q[:, :, 1], ALU.add))
                ch.do(ve.tensor_tensor(g_d[:, :], q[:, :, 2], q[:, :, 3], ALU.add))
                ch.sync()
                ch.do(ve.tensor_tensor(g_a[:, :], g_a[:, :], g_b[:, :], ALU.add))
                ch.do(ve.tensor_tensor(g_c[:, :], g_c[:, :], g_d[:, :], ALU.max))
                ch.sync()
                ch.do(ve.tensor_tensor(g_a[:, :], g_a[:, :], g_c[:, :], ALU.max))
                ga = g_a[:, :].rearrange("p (t g) -> p t g", t=NT)
                ch.sync()
                carry(ve, 1)
                for j in range(NT):
                    ch.do(ve.max(g_top[:, j, :], ga[:, j, :]))
                ch.sync()
                carry(ve, 1)
                for j in range(NT):
                    ch.do(ve.max_index(g_idx[:, j, :], g_top[:, j, :], ga[:, j, :]))
                ch.sync()
                ch.link(ve.tensor_copy(g_idf[:, :, :], g_idx[:, :, :]))
                ch.link(ve.tensor_tensor(g_eq[:, :, :, :],
                                         iota_e[:, 0:NGRP].unsqueeze(1).unsqueeze(1).to_broadcast([P, NT, TOPG, NGRP]),
                                         g_idf[:, :, 0:TOPG].unsqueeze(3).to_broadcast([P, NT, TOPG, NGRP]),
                                         ALU.is_equal))
                ch.link(ve.tensor_reduce(g_b[:, :].rearrange("p (t g) -> p t g", t=NT),
                                         g_eq[:, :, :, :].rearrange("p t k g -> p t g k"), AX.X, ALU.add))
                ch.link(ve.tensor_tensor(masked[:, :, :].rearrange("p t (g i) -> p (t g) i", i=EPG), q,
                                         g_b[:, :].unsqueeze(2).to_broadcast([P, NT * NGRP, EPG]), ALU.mult))
                ch.do(ve.tensor_scalar(masked[:, :, :], masked[:, :, :], 0.0, None, ALU.add))
                ch.sync()
                carry(ve, 1)
                for j in range(NT):
                    ch.do(ve.max(e_top[:, j, :], masked[:, j, :]))
                ch.sync()
                carry(ve, 1)
                for j in range(NT):
                    ch.do(ve.max_index(e_idx[:, j, :], e_top[:, j, :], masked[:, j, :]))
                ch.sync()
                ch.link(ve.tensor_copy(e_idf[:, :, :], e_idx[:, :, 0:TOPK]))
                ch.link(ve.tensor_tensor(e_eq[:, :, :, :],
                                         iota_e[:, :].unsqueeze(1).unsqueeze(1).to_broadcast([P, NT, TOPK, E]),
                                         e_idf[:, :, :].unsqueeze(3).to_broadcast([P, NT, TOPK, E]), ALU.is_equal))
                with nc.allow_low_precision(reason="zeros and ones"):
                    ve.tensor_reduce(picks[:, :, :], e_eq[:, :, :, :].rearrange("p t k e -> p t e k"), AX.X,
                                     ALU.add).then_inc(d_picks, 1)
                ch.link(ve.tensor_tensor(e_pr[:, :, :, :], e_eq[:, :, :, :],
                                         s_sb[:, :, :].unsqueeze(2).to_broadcast([P, NT, TOPK, E]), ALU.mult))
                ch.link(ve.tensor_reduce(r_w[:, :, :], e_pr[:, :, :, :], AX.X, ALU.add))
                ch.link(ve.tensor_reduce(r_den[:, :], r_w[:, :, :], AX.X, ALU.add))
                ch.link(ve.tensor_scalar(r_den[:, :], r_den[:, :], 1e-20, None, ALU.add))
                ch.link(ve.reciprocal(r_den[:, :], r_den[:, :]))
                ch.link(ve.tensor_tensor(r_w[:, :, :], r_w[:, :, :], r_den[:, :].unsqueeze(2).to_broadcast([P, NT, TOPK]),
                                         ALU.mult))

            def route_slots(g):
                dve.wait_ge(pe_pos, g + 1)
                ch.link(ve.tensor_tensor(e_pr[:, :, :, :], e_eq[:, :, :, :],
                                         pos_ps.unsqueeze(2).to_broadcast([P, NT, TOPK, E]), ALU.mult))
                ch.link(ve.tensor_reduce(r_pos[:, :, :], e_pr[:, :, :, :], AX.X, ALU.add))
                ch.do(ve.tensor_scalar(r_ge[:, :, :], r_pos[:, :, :], float(C), NO_SLOT, ALU.is_ge, ALU.mult))
                ch.do(ve.scalar_tensor_tensor(out=r_pos[:, :, :], in0=e_idf[:, :, :], scalar=float(C),
                                              in1=r_pos[:, :, :], op0=ALU.mult, op1=ALU.add))
                ch.do(ve.tensor_tensor(cum[:, :], cum[:, :], picks[:, 0, :], ALU.add))
                ch.sync()
                wait(dve, st_slot, g * (16 * NT * TOPK))
                ch.do(ve.tensor_tensor(dest[:, :].rearrange("p (t k) -> p t k", t=NT), r_pos[:, :, :], r_ge[:, :, :],
                                       ALU.add))
                ch.do(ve.tensor_scalar(payload[:, :, 1].rearrange("p (t k) -> p t k", t=NT), r_w[:, :, :],
                                       ROUTED_SCALE, None, ALU.mult))
                ch.do(ve.tensor_copy(payload[:, :, 0].rearrange("p (t k) -> p t k", t=NT),
                                     tokid[:, :].unsqueeze(2).to_broadcast([P, NT, TOPK])))
                ch.link(ve.tensor_tensor(cum[:, :], cum[:, :], picks[:, 1, :], ALU.add))
                ch.do(ve.tensor_scalar(tokid[:, :], tokid[:, :], float(G), None, ALU.add))
                ch.do(ve.tensor_copy(cumb[:, :], cum[:, :]))
                ch.sync()
                ve.tensor_copy(sc1[:, 10:11], sc1[:, 9:10]).then_inc(d_route, 1)

            def add_shared(g, r, u):
                j, h = u // 2, u % 2
                at = xbuf[r][:, j, h * HALF:(h + 1) * HALF]
                dve.wait_ge(pe_dn, 4 * g + u + 1)
                ve.scalar_tensor_tensor(out=at, in0=PS[4 + u % 2][:, :], scalar=DOWN_PROJ, in1=at, op0=ALU.mult,
                                        op1=ALU.add).then_inc(d_out, 1)

            def group(g, r, front=True, ctx_piece=True, weights=None):
                for ic in range(KS):
                    n = 8 * g + ic
                    bank = PS[ic % 2]
                    dve.wait_ge(a_sig, n + 1)
                    ve.scalar_tensor_tensor(out=gup, in0=bank[:, G:2 * G], scalar=H_SCALE * UP_PROJ * UP_PROJ,
                                            in1=sig[ic % 2], op0=ALU.mult, op1=ALU.mult).then_inc(d_t, 1)
                    dve.wait_ge(d_t, n + 1)
                    wait(dve, a_hh, 8 * g + (ic - 1 if ic > 1 else 0))
                    ve.tensor_tensor(h32[ic % 2], gup, bank[:, 0:G], ALU.mult).then_inc(d_h, 1)
                    if ic == 1:
                        route_picks(g)
                    if front and ic in (2, 3):
                        x_round(g + 1, ic - 2, M_main)
                    if ctx_piece and ic in (4, 5):
                        j = ic - 4
                        dve.wait_ge(a_cv, 2 * g + 8 + j + 1)
                        tile = (2 * g + 8 + j) & 15
                        wait(dve, pe_xa, 4 * g + 4)
                        fp8_round(ctx_ring[j], M_main, BIG[:, bass.ds(tile * D, D)]).then_inc(d_cq, 1)
                    if ic == 6:
                        route_slots(g)
                    dve.wait_ge(a_hh, n + 1)
                    ve.tensor_tensor(hT[1][:, ic, :], h32[ic % 2], hT[0][:, ic, :], ALU.subtract).then_inc(d_hl, 1)
                if front:
                    residual(g + 1, 1 - r)
                    shift(g + 1)
                if weights:
                    weights(0)
                add_shared(g, r, 0)
                if weights:
                    weights(1)
                add_shared(g, r, 1)
                if front:
                    xt_lo(g + 1, 0)
                if weights:
                    weights(2)
                add_shared(g, r, 2)
                if front:
                    xt_lo(g + 1, 1)
                if weights:
                    weights(3)
                add_shared(g, r, 3)

            ch.close()
            STEPS = GROUP_STEPS
            base = ch.before
            group(0, 0)
            group(1, 1)
            with dve.Fori(1, 6) as pair:
                for r in range(2):
                    ch.before, ch.n = pair * (2 * STEPS) + (base + r * STEPS), 0
                    group(pair * 2 + r, r)
                    assert ch.n == STEPS, ch.n
            ch.before, ch.n = base + 12 * STEPS, 0

            def ew_lo(e, b, m):
                dve.wait_ge(x_hi, e * 6 + (m + 1))
                stage = ew_stage[m]
                k = 4 if m < 4 else 2
                src = stage.rearrange("p (k i) -> p k i", k=k)
                cut = (slice(None), slice((m % 2) * k, (m % 2) * k + k), slice(None))
                hi, lo = EW[b][m // 2]
                ve.scalar_tensor_tensor(out=lo[cut], in0=src, scalar=W_SCALE, in1=hi[cut], op0=ALU.mult,
                                        op1=ALU.subtract).then_inc(x_lo, 1)

            def et_lo(e):
                for s in range(3):
                    k = 3 if s < 2 else 2
                    dve.wait_ge(x_xh, e * 3 + (s + 1))
                    ve.scalar_tensor_tensor(out=eT[1][:, 3 * s:3 * s + k, :],
                                            in0=PS[(2, 3, 6)[s]][:, 0:k * C].rearrange("p (k t) -> p k t", k=k),
                                            scalar=X_SCALE, in1=eT[0][:, 3 * s:3 * s + k, :], op0=ALU.mult,
                                            op1=ALU.subtract).then_inc(x_xl, 1)

            for g in range(12, GROUPS):
                last = g == GROUPS - 1
                group(g, g % 2, front=not last, ctx_piece=False,
                      weights=(lambda n: ew_lo(0, 0, n)) if last else None)
            ew_lo(0, 0, 4)
            et_lo(0)

            def expert(e, b, more=True):
                for ic in range(KI):
                    bank = PS[ic % 2]
                    dve.wait_ge(x_sig, e * 4 + (ic + 1))
                    ve.scalar_tensor_tensor(out=gup[:, 0:C], in0=bank[:, G:G + C], scalar=H_SCALE * UP_PROJ * UP_PROJ,
                                            in1=sig[ic % 2][:, 0:C], op0=ALU.mult, op1=ALU.mult).then_inc(x_t, 1)
                    dve.wait_ge(x_t, e * 4 + (ic + 1))
                    wait(dve, x_hh, e * 4 + (ic - 1 if ic > 1 else 0))
                    ve.tensor_tensor(h32[ic % 2][:, 0:C], gup[:, 0:C], bank[:, 0:C], ALU.mult).then_inc(x_h, 1)
                    dve.wait_ge(x_hh, e * 4 + (ic + 1))
                    ve.tensor_tensor(ehT[1][:, ic, :], h32[ic % 2][:, 0:C], ehT[0][:, ic, :],
                                     ALU.subtract).then_inc(x_hl, 1)
                    if ic == 0:
                        ew_lo(e, b, 5)
                    elif more and ic < 3:
                        ew_lo(e + 1, 1 - b, ic - 1)
                if more:
                    et_lo(e + 1)
                    for m in range(2, 5):
                        ew_lo(e + 1, 1 - b, m)

            expert(0, 0)
            expert(1, 1)
            with dve.Fori(1, E // 2 - 1) as pair:
                expert(pair * 2, 0)
                expert(pair * 2 + 1, 1)
            expert(E - 2, 0)
            expert(E - 1, 1, more=False)

        @block.tensor
        def _(pe):
            te = nc.tensor

            def product(out_ps, weights, data, chunks, cols):
                (whi, wlo), (xhi, xlo) = weights, data
                steps = [(a, b, k) for k in range(chunks) for a, b in ((whi, xhi), (whi, xlo), (wlo, xhi))]
                for n, (a, b, k) in enumerate(steps):
                    ins = te.matmul(out_ps, a[:, k, cols], b[:, k, :], start=n == 0, stop=n == len(steps) - 1)
                return ins

            def down(out_ps, acts, weights, chunks, toks, cols):
                (hhi, hlo), (whi, wlo) = acts, weights
                steps = [(a, b, k) for k in range(chunks) for a, b in ((hhi, whi), (hhi, wlo), (hlo, whi))]
                for n, (a, b, k) in enumerate(steps):
                    ins = te.matmul(out_ps, a[:, k, toks], b[:, k, cols], start=n == 0, stop=n == len(steps) - 1)
                return ins

            def xq_transpose(f):
                wait(pe, d_xl, 4 * f)
                for j in range(NT):
                    pe.wait_ge(d_q, 2 * f + j + 1)
                    bank = PS[6 + j][:, :].bitcast(BF16)
                    for k in range(KD):
                        ins = te.transpose(bank[:, k * P:(k + 1) * P], xq[j][:, k * P:(k + 1) * P], identb[:, :])
                    ins.then_inc(pe_xq, 1)

            def cross(f):
                batch = f >> 2
                pe.wait_ge(d_cq, batch * 8 + 8)
                wait(pe, a_lg, f)
                wait(pe, d_route, f)
                for j in range(NT):
                    pe.wait_ge(a_xq, 2 * f + j + 1)
                    for h in range(2):
                        if j:
                            pe.wait_ge(d_x2, 4 * f + h + 1)
                        for k in range(KD):
                            ctx_at = (batch & 1) * (8 * D) + (k * D + h * HALF)
                            ins = te.matmul(PS[2 + h][:, :], xqT[:, k, j * P:(j + 1) * P], BIG[:, bass.ds(ctx_at, HALF)],
                                            start=k == 0, stop=k == KD - 1)
                        ins.then_inc(pe_xa, 1)

            def xt_transpose(f, j):
                pe.wait_ge(a_xn, 2 * f + j + 1)
                for h in range(2):
                    if j == 0:
                        pe.wait_ge(a_xq, 2 * f + h + 1)
                    else:
                        pe.wait_ge(d_xl, 4 * f + h + 1)
                    for k in range(4):
                        ins = te.transpose(PS[6 + h][:, k * P:(k + 1) * P], xn[j][:, (4 * h + k) * P:(4 * h + k + 1) * P],
                                           identf[:, :])
                    ins.then_inc(pe_xt, 1)

            def group(g, r, front=True):
                pe.wait_ge(d_xl, 4 * g + 4)
                for ic in range(KS):
                    wait(pe, d_h, 8 * g + (ic - 1 if ic > 1 else 0))
                    cols = slice(ic * P, (ic + 1) * P)
                    product(PS[ic % 2][:, 0:G], SW[0], xT, KD, cols)
                    product(PS[ic % 2][:, G:2 * G], SW[1], xT, KD, cols).then_inc(pe_gu, 1)
                    if ic == 0:
                        pe.wait_ge(d_x2, 4 * g + 4)
                        for k in range(KD):
                            for v in range(2):
                                ins = te.matmul(logit_ps, rw[:, k, :], xT[v][:, k, :], start=k + v == 0,
                                                stop=k == KD - 1 and v == 1)
                        ins.then_inc(pe_lg, 1)
                    if ic == 1:
                        pe.wait_ge(a_lg, g + 1)
                        for j in range(NT):
                            ins = te.matmul(score_ps[:, j * E:(j + 1) * E], lg[:, j * P:(j + 1) * P], sel[:, :],
                                            start=True, stop=True)
                        ins.then_inc(pe_lt, 1)
                    if ic == 5:
                        pe.wait_ge(d_picks, g + 1)
                        pe.wait_ge(a_sc, g + 1)
                        wait(pe, d_route, g)
                        te.matmul(pos_ps[:, 0, :], tri[:, :], picks[:, 0, :], start=True, stop=False)
                        te.matmul(pos_ps[:, 0, :], ones[:, :], cumb[:, :], start=False, stop=True)
                        te.matmul(pos_ps[:, 1, :], tri[:, :], picks[:, 1, :], start=True, stop=False)
                        te.matmul(pos_ps[:, 1, :], ones[:, :], picks[:, 0, :], start=False, stop=False)
                        te.matmul(pos_ps[:, 1, :], ones[:, :], cumb[:, :], start=False, stop=True).then_inc(pe_pos, 1)
                    if front and ic == 6:
                        xq_transpose(g + 1)
                if front:
                    cross(g + 1)
                pe.wait_ge(d_hl, 8 * g + 8)
                for u in range(4):
                    j, h = u // 2, u % 2
                    wait(pe, d_out, 4 * g + (u - 1 if u > 1 else 0))
                    if front and u in (2, 3):
                        xt_transpose(g + 1, u - 2)
                    down(PS[4 + u % 2][:, :], hT, SW[2], KS, slice(j * P, (j + 1) * P),
                         slice(h * HALF, (h + 1) * HALF)).then_inc(pe_dn, 1)

            pe.wait_ge(consts_ready, 2)
            xq_transpose(0)
            cross(0)
            xt_transpose(0, 0)
            xt_transpose(0, 1)
            pe.wait_ge(rw_lo, 1)
            pe.wait_ge(sw_lo, 12)
            group(0, 0)
            group(1, 1)
            with pe.Fori(1, 6) as pair:
                group(pair * 2, 0)
                group(pair * 2 + 1, 1)
            for g in range(12, GROUPS):
                group(g, g % 2, front=g < GROUPS - 1)

            def et_transpose(e, b):
                pe.wait_ge(ld_xg[b], (e - b) * 16 + 32)
                for s in range(3):
                    for k in range(3 if s < 2 else 2):
                        for blk in range(2):
                            kk = 3 * s + k
                            ins = te.transpose(PS[(2, 3, 6)[s]][:, k * C + blk * HC:k * C + (blk + 1) * HC],
                                               xg[b][:, blk, kk * P:(kk + 1) * P], identf[0:HC, 0:HC])
                    ins.then_inc(x_xt, 1)

            pe.wait_ge(a_lg, GROUPS)
            pe.wait_ge(d_route, GROUPS)
            et_transpose(0, 0)
            pe.wait_ge(d_h, 8 * GROUPS)
            pe.wait_ge(d_out, 4 * GROUPS)

            def expert(e, b, more=True):
                pe.wait_ge(x_lo, e * 6 + 4)
                pe.wait_ge(x_xl, e * 3 + 3)
                for ic in range(KI):
                    wait(pe, x_h, e * 4 + (ic - 1 if ic > 1 else 0))
                    cols = slice(ic * P, (ic + 1) * P)
                    product(PS[ic % 2][:, 0:C], EW[b][0], eT, KD, cols)
                    product(PS[ic % 2][:, G:G + C], EW[b][1], eT, KD, cols).then_inc(x_gu, 1)
                if more:
                    et_transpose(e + 1, 1 - b)
                pe.wait_ge(x_lo, e * 6 + 6)
                pe.wait_ge(x_hl, e * 4 + 4)
                for u in range(4):
                    blk, h = u // 2, u % 2
                    wait(pe, x_y, e * 4 + (u - 1 if u > 1 else 0))
                    down(PS[4 + u % 2][0:HC, :], ehT, EW[b][2], KI, slice(blk * HC, (blk + 1) * HC),
                         slice(h * HALF, (h + 1) * HALF)).then_inc(x_dn, 1)

            expert(0, 0)
            expert(1, 1)
            with pe.Fori(1, E // 2 - 1) as pair:
                expert(pair * 2, 0)
                expert(pair * 2 + 1, 1)
            expert(E - 2, 0)
            expert(E - 1, 1, more=False)


GROUP_STEPS = 62


def kernel(**inputs):
    import concourse.bacc as bacc
    from concourse.bass_utils import run_bass_kernel_spmd

    a = {k: np.asarray(v) for k, v in inputs.items()}
    T, D = 4096, 1024
    data = {
        "x": a["x"].reshape(T, D),
        "ctx_in": a["ctx_2048"].reshape(T, D),
        "mask": a["mask_Bx1xS2_ff0"].reshape(4, D),
        "router_t": a["L0_ffn_router_w"].T,
        "e_bias": a["L0_ffn_e_bias"],
        "w_gate": a["L0_ffn_W_gate"].reshape(32 * 1024, 512),
        "w_up": a["L0_ffn_W_up"].reshape(32 * 1024, 512),
        "w_down": a["L0_ffn_W_down"].reshape(32 * 512, 1024),
        "sh_gate": a["L0_ffn_shared_gate"].T,
        "sh_up": a["L0_ffn_shared_up"].T,
        "sh_down": a["L0_ffn_shared_down"].T,
    }
    nc = bacc.Bacc("TRN2", target_bir_lowering=False, num_devices=1)
    arrays, args = {}, []
    for name, v in data.items():
        v = np.ascontiguousarray(v)
        arrays[f"in_{name}"] = v
        args.append(nc.dram_tensor(f"in_{name}", v.shape, mybir.dt.from_np(v.dtype), kind="ExternalInput").ap())
    args.append(nc.dram_tensor("out_rows", (T + 160, D), F32, kind="ExternalOutput").ap())
    args.append(nc.dram_tensor("xn_rows", (T, D), F32).ap())
    args.append(nc.dram_tensor("slots", (32 * 160, 2), F32).ap())
    moe_kernel(nc, *args)
    r = run_bass_kernel_spmd(nc, [arrays], core_ids=[0])
    return r.results[0]["out_rows"][:T].reshape(4, 1024, 1024)
```

```python
from contextlib import ExitStack

import numpy as np

import concourse.bass as bass
from concourse import mybir

ALU = mybir.AluOpType
ACT = mybir.ActivationFunctionType
AX = mybir.AxisListType
F32 = mybir.dt.float32
F16 = mybir.dt.float16
BF16 = mybir.dt.bfloat16
I32 = mybir.dt.int32
U32 = mybir.dt.uint32

P = 128
LN_EPS = 1e-5
FP8_MAX = 448.0
EXPONENT_BITS = 0x7F800000
FP8_MIN_NORMAL = 2.0 ** -6
ROUNDER = 1.5 * 2.0 ** 20

X_SCALE = 2.0 ** 10
W_SCALE = 2.0 ** 4
H_SCALE = 2.0 ** -2
UP_PROJ = 1.0 / (X_SCALE * W_SCALE)
DOWN_PROJ = 1.0 / (H_SCALE * W_SCALE)
NO_SLOT = 1.0e6
ROUTED_SCALE = 2.5


def moe_kernel(nc, x, ctx_in, mask, router_t, e_bias, w_gate, w_up, w_down, sh_gate, sh_up, sh_down, out,
               xn_dram, slot_dram):
    T, D = x.shape
    E = router_t.shape[1]
    I = w_gate.shape[1]
    SI = sh_gate.shape[1]
    TOPK, NGRP, TOPG = 4, 8, 3
    EPG = E // NGRP
    C = -(-(5 * T) // (4 * E))
    HC = C // 2
    G = 256
    NT = G // P
    GROUPS = T // G
    KD = D // P
    KS = SI // P
    KI = I // P
    BATCH_TILES = 8
    HALF = 512
    CH = 4
    XCHUNKS = T // (CH * P)
    CCHUNKS = XCHUNKS - 2
    COLS = 2 * E

    with ExitStack() as stack:
        def sb(name, shape, dt):
            return stack.enter_context(nc.sbuf_tensor(name, shape, dt))

        def sem(name):
            return stack.enter_context(nc.semaphore(name))

        W = sb("W", [P, 49152], F16)
        BIG = sb("BIG", [P, 24576], BF16)
        X = sb("X", [P, 2 * NT * D], F32)
        FR = sb("FR", [P, 4096], F32)
        XT = sb("XT", [P, 2 * KD * G], F16)
        HH = sb("HH", [P, 2 * KS * G], F16)
        SG = sb("SG", [P, 5 * G], F32)

        identf = sb("identf", [P, P], F32)
        identb = sb("identb", [P, P], BF16)
        tri = sb("tri", [P, P], BF16)
        ones = sb("ones", [P, P], BF16)
        rw = sb("rw", [P, KD, 2 * E], F16)
        sel = sb("sel", [2 * E, E], F32)
        bias_sb = sb("bias_sb", [P, E], F32)
        lg = sb("lg", [2 * E, G], F32)
        iota_e = sb("iota_e", [P, E], F32)
        tokid = sb("tokid", [P, NT], F32)
        expo = sb("expo", [P, 4], F32)
        a1 = sb("a1", [P, T // P], F32)
        b1 = sb("b1", [P, T // P], F32)
        st1 = sb("st1", [P, CH, 2, 6], F32)
        mv1 = sb("mv1", [P, CH, 2], F32)
        ve1 = sb("ve1", [P, CH], F32)
        amax = sb("amax", [P, XCHUNKS + CCHUNKS + 4], F32)
        sc1 = sb("sc1", [P, 16], F32)
        st2 = sb("st2", [P, NT, 2, 6], F32)
        mv2 = sb("mv2", [P, NT, 2], F32)
        ve2 = sb("ve2", [P, NT], F32)
        rs2 = sb("rs2", [P, NT], F32)
        nb2 = sb("nb2", [P, NT], F32)
        s_sb = sb("s_sb", [P, NT, E], F32)
        sc = sb("sc", [P, NT, E], F32)
        masked = sb("masked", [P, NT, E], F32)
        g_a = sb("g_a", [P, NT * NGRP], F32)
        g_b = sb("g_b", [P, NT * NGRP], F32)
        g_c = sb("g_c", [P, NT * NGRP], F32)
        g_d = sb("g_d", [P, NT * NGRP], F32)
        g_top = sb("g_top", [P, NT, 8], F32)
        g_idx = sb("g_idx", [P, NT, 8], U32)
        g_idf = sb("g_idf", [P, NT, 8], F32)
        g_eq = sb("g_eq", [P, NT, TOPG, NGRP], F32)
        e_top = sb("e_top", [P, NT, 8], F32)
        e_idx = sb("e_idx", [P, NT, 8], U32)
        e_idf = sb("e_idf", [P, NT, TOPK], F32)
        e_eq = sb("e_eq", [P, NT, TOPK, E], F32)
        e_pr = sb("e_pr", [P, NT, TOPK, E], F32)
        r_w = sb("r_w", [P, NT, TOPK], F32)
        r_den = sb("r_den", [P, NT], F32)
        r_pos = sb("r_pos", [P, NT, TOPK], F32)
        r_ge = sb("r_ge", [P, NT, TOPK], F32)
        picks = sb("picks", [P, NT, E], BF16)
        cum = sb("cum", [P, E], F32)
        cumb = sb("cumb", [P, E], BF16)
        dest = sb("dest", [P, NT * TOPK], U32)
        payload = sb("payload", [P, NT * TOPK, 2], F32)
        tab = sb("tab", [HC, COLS, 2], F32)
        gidx = sb("gidx", [HC, COLS], U32)
        sidx = sb("sidx", [HC, COLS], U32)
        wts = sb("wts", [HC, COLS], F32)
        gix = sb("gix", [HC, 4], U32)
        six = sb("six", [HC, 4], U32)

        PS = [stack.enter_context(nc.psum_tensor(f"ps{i}", [P, 512], F32)) for i in range(8)]

        def wview(at, k, n):
            return W[:, at:at + k * n].rearrange("p (k n) -> p k n", k=k)

        SW = [[wview((2 * m + v) * 8192, 8, 1024) for v in range(2)] for m in range(3)]
        EW = [[[wview(b * 24576 + (2 * m + v) * 4096, KI if m == 2 else KD, D if m == 2 else I) for v in range(2)]
               for m in range(3)] for b in range(2)]
        p1_slot = [W[:, s * 8192:(s + 1) * 8192].bitcast(F32) for s in range(4)]
        sw_stage = [W[:, 32768 + 4096 * s:32768 + 4096 * (s + 1)].bitcast(F32) for s in range(4)]
        sd_stage = [BIG[:, 10240 + 2048 * s:10240 + 2048 * (s + 1)].bitcast(F32) for s in range(3)]
        ctx0 = [BIG[:, 8192 + 4096 * m:8192 + 4096 * (m + 1)].bitcast(F32) for m in range(4)]
        ctx_ring = [BIG[:, 16384 + 2048 * s:16384 + 2048 * (s + 1)].bitcast(F32) for s in range(2)]
        mask_sb = BIG[:, 20480:22528].bitcast(F32)
        mask_first = X[:, 3 * D:4 * D]
        M_main = BIG[:, 22528:24576].bitcast(F32)
        M_first = XT[:, :].bitcast(F32)
        ew_stage = [BIG[:, 4096 * m:4096 * (m + 1)].bitcast(F32) for m in range(6)]
        xbuf = [X[:, b * NT * D:(b + 1) * NT * D].rearrange("p (t d) -> p t d", t=NT) for b in range(2)]
        xn = [FR[:, j * D:(j + 1) * D] for j in range(NT)]
        xqT = FR[:, 2048:3072].bitcast(BF16).rearrange("p (k t) -> p k t", k=KD)
        xq = [FR[:, 3072 + 512 * j:3072 + 512 * (j + 1)].bitcast(BF16) for j in range(NT)]
        xT = [XT[:, v * KD * G:(v + 1) * KD * G].rearrange("p (k t) -> p k t", k=KD) for v in range(2)]
        hT = [HH[:, v * KS * G:(v + 1) * KS * G].rearrange("p (k t) -> p k t", k=KS) for v in range(2)]
        eT = [XT[:, v * KD * G:v * KD * G + KD * C].rearrange("p (k t) -> p k t", k=KD) for v in range(2)]
        ehT = [HH[:, v * KS * G:v * KS * G + KI * C].rearrange("p (k t) -> p k t", k=KI) for v in range(2)]
        sig = [SG[:, b * G:(b + 1) * G] for b in range(2)]
        h32 = [SG[:, (2 + b) * G:(3 + b) * G] for b in range(2)]
        gup = SG[:, 4 * G:5 * G]
        rw_f = SG[:, 0:KD * E].rearrange("p (k e) -> p k e", k=KD)
        zeros = HH[0:HC, :].bitcast(F32)
        slot_init = FR[0:E, 0:2 * C].rearrange("p (s w) -> p s w", s=C)
        ybuf = [X[0:HC, b * 2048:(b + 1) * 2048].rearrange("p (t d) -> p t d", t=2) for b in range(2)]
        xg = [FR[0:HC, b * 2048:(b + 1) * 2048].rearrange("p (t d) -> p t d", t=2) for b in range(2)]
        yT = [HH[:, h * KS * G + KI * C:h * KS * G + KI * C + 8 * C].bitcast(F32).rearrange("p (k t) -> p k t", k=4)
              for h in range(2)]
        DOWN_BANKS = (4, 5, 7, 4)
        ROW_BANKS = (2, 3, 6, 7)
        DOWN_ORDER = [(q, 0, k) for q in range(3) for k in range(KI - 1)]
        for q in range(4):
            DOWN_ORDER += [(q, 0, k) for k in range(KI - 1 if q < 3 else 0, KI)] + [(q, 1, k) for k in range(KI)]
        logit_ps = PS[2][0:2 * E, 0:G]
        score_ps = PS[3][:, 0:NT * E]
        pos_ps = PS[3][:, 64:64 + NT * E].rearrange("p (t e) -> p t e", t=NT)

        ld_small = sem("ld_small")
        ld_first = [sem(f"ld_first{t}") for t in range(2 * CH)]
        ld_p1 = [sem(f"ld_p1_{s}") for s in range(4)]
        ld_c0 = [sem(f"ld_c0_{m}") for m in range(4)]
        ld_sw = [sem(f"ld_sw{s}") for s in range(7)]
        ld_x = [sem(f"ld_x{b}") for b in range(2)]
        ld_mask = sem("ld_mask")
        ld_ctx = [sem(f"ld_ctx{b}") for b in range(2)]
        ld_tab = sem("ld_tab")
        ld_ew = [sem(f"ld_ew{m}") for m in range(6)]
        ld_xg = [sem(f"ld_xg{b}") for b in range(2)]
        st_init = sem("st_init")
        st_xn = [sem(f"st_xn{j}") for j in range(NT)]
        st_out = [sem(f"st_out{b}") for b in range(2)]
        st_slot = sem("st_slot")
        st_y = [sem(f"st_y{b}") for b in range(2)]
        consts_ready = sem("consts_ready")
        pool_step = sem("pool_step")
        ve1_ready, rs1_ready, nb1_ready, ln1_done, p1_done = map(sem, ("ve1_ready", "rs1_ready", "nb1_ready", "ln1_done", "p1_done"))
        amax_ready, amax_all, scales_ready = map(sem, ("amax_ready", "amax_all", "scales_ready"))
        sw_hi, sw_lo, rw_hi, rw_lo = map(sem, ("sw_hi", "sw_lo", "rw_hi", "rw_lo"))
        pe_gu, pe_xq, pe_xa, pe_xt, pe_dn, pe_lg, pe_lt, pe_pos = map(
            sem, ("pe_gu", "pe_xq", "pe_xa", "pe_xt", "pe_dn", "pe_lg", "pe_lt", "pe_pos"))
        a_v, a_cv, a_xq, a_xn, a_xh, a_sig, a_hh, a_lg, a_sc = map(
            sem, ("a_v", "a_cv", "a_xq", "a_xn", "a_xh", "a_sig", "a_hh", "a_lg", "a_sc"))
        d_q, d_cq, d_x2, d_var, d_nb, d_xl, d_t, d_h, d_hl, d_out, d_picks, d_route, d_chain = map(
            sem, ("d_q", "d_cq", "d_x2", "d_var", "d_nb", "d_xl", "d_t", "d_h", "d_hl", "d_out", "d_picks",
                  "d_route", "d_chain"))
        p_xm, p_rs, p_carry = map(sem, ("p_xm", "p_rs", "p_carry"))
        x_gu, x_xt, x_dn, x_yt, x_tr, x_hi, x_lo, x_sig, x_hh, x_xh, x_y, x_t, x_h, x_hl, x_xl = map(
            sem, ("x_gu", "x_xt", "x_dn", "x_yt", "x_tr", "x_hi", "x_lo", "x_sig", "x_hh", "x_xh", "x_y", "x_t", "x_h",
                  "x_hl", "x_xl"))

        def wait(eng, s, value):
            if isinstance(value, int) and value <= 0:
                return
            eng.wait_ge(s, value)

        def settle(eng):
            eng.wait_ge(consts_ready, 2)

        def carry(engine, col):
            return engine.tensor_tensor(expo[:, col:col + 1], expo[:, 0:1], expo[:, 0:1], ALU.add)

        class Chain:

            def __init__(self, eng, s):
                self.eng, self.s, self.before, self.n = eng, s, 0, 0

            def do(self, ins):
                ins.then_inc(self.s, 1)
                self.n += 1

            def sync(self):
                self.eng.wait_ge(self.s, self.before + self.n)

            def link(self, ins):
                self.do(ins)
                self.sync()

            def close(self):
                self.before, self.n = self.before + self.n, 0

        SW_PIECES = [(m, k, 4, ih) for ih in range(2) for m in range(2) for k in (0, 4)]
        SW_PIECES += [(2, k, 2, nh) for nh in range(2) for k in (0, 2, 4, 6)]
        FIRST_SPLITS = [(4, 5), (6, 7), (), (), (), (8, 9), (10,), (11, 12), (13, 14, 15)]
        sw_dram = [sh_gate, sh_up, sh_down]

        def p1_loads(c):
            return c // 4 + (c % 4 > 1)

        def sw_slot(n):
            return (n % 4, sw_stage[n % 4]) if n < 8 else (4 + (n - 8) % 3, sd_stage[(n - 8) % 3])

        def sw_uses(n):
            return n // 4 + 1 if n < 8 else (n - 8) // 3 + 1

        def rows(dram, start, count):
            return dram[bass.ds(start, count), :]

        block = stack.enter_context(nc.Block())

        @block.sync
        def _(sp):
            def p1_load(c):
                wait(sp, p1_done, c - 3)
                src, r = (x, c * CH * P) if c < XCHUNKS else (ctx_in, (c - XCHUNKS + 2) * CH * P)
                if c < 2:
                    for t in range(CH):
                        at = (c * CH + t) * P
                        sp.dma_start(p1_slot[c][:, t * D:(t + 1) * D], x[at:at + P, :]).then_inc(ld_first[c * CH + t], 16)
                    return
                sp.dma_start(p1_slot[c % 4].rearrange("p (t d) -> p t d", t=CH),
                             src[r:r + CH * P, :].rearrange("(t p) d -> p t d", p=P)).then_inc(ld_p1[c % 4], 16)

            def sw_load(n):
                s, stage = sw_slot(n)
                if n < 8:
                    wait(sp, sw_lo, n - 3)
                elif n < 11:
                    wait(sp, d_cq, n - 6)
                else:
                    wait(sp, sw_lo, n - 2)
                m, k0, k, ih = SW_PIECES[n]
                sp.dma_start(stage.rearrange("p (k i) -> p k i", k=k),
                             sw_dram[m][k0 * P:(k0 + k) * P, ih * 512:(ih + 1) * 512]
                             .rearrange("(k p) i -> p k i", p=P)).then_inc(ld_sw[s], 16)

            def x_load(f, b):
                sp.dma_start(xbuf[b], rows(x, f * G, G).rearrange("(t p) d -> p t d", p=P)).then_inc(ld_x[b], 16)

            def ctx_load(t, slot):
                sp.dma_start(ctx_ring[slot], rows(ctx_in, t * P, P)).then_inc(ld_ctx[slot], 16)

            def mask_load(f):
                sp.dma_start(mask_first if isinstance(f, int) and f == 0 else mask_sb, rows(mask, f >> 2, 1).squeeze(0).partition_broadcast(P)).then_inc(ld_mask, 16)

            for c in range(XCHUNKS):
                p1_load(c)
                if c == 3:
                    sp.wait_ge(consts_ready, 2)
                    sp.dma_start(out[T:T + C, :].rearrange("(t p) d -> p t d", p=HC),
                                 zeros.rearrange("p (t d) -> p t d", t=2)).then_inc(st_init, 16)
                    sp.dma_start(slot_dram.rearrange("(e s) w -> e s w", e=E), slot_init).then_inc(st_init, 16)

            x_load(0, 0)
            mask_load(0)
            for c in range(XCHUNKS, XCHUNKS + CCHUNKS):
                p1_load(c)
            for m in range(4):
                sp.dma_start(ctx0[m].rearrange("p (t d) -> p t d", t=2),
                             ctx_in[m * 256:(m + 1) * 256, :].rearrange("(t p) d -> p t d", p=P)).then_inc(ld_c0[m], 16)
            for n in range(4):
                sw_load(n)
            for n in range(4, 11):
                sw_load(n)
            ctx_load(9, 1)
            ctx_load(8, 0)

            def xn_stores(f):
                for j in range(NT):
                    wait(sp, a_xn, 2 * f + j + 1)
                    sp.dma_start(rows(xn_dram, f * G + j * P, P), xn[j]).then_inc(st_xn[j], 16)

            def group(g, r, front=True, ctx=2):
                first = isinstance(g, int) and g == 0
                if front:
                    if first:
                        wait(sp, p_xm, 2)
                    wait(sp, st_out[1 - r], (g + r) * 16)
                    x_load(g + 1, 1 - r)
                    wait(sp, p_xm, 2 * g + 2)
                    if first:
                        wait(sp, d_cq, 8)
                    mask_load(g + 1)
                if first:
                    for n in range(11, 16):
                        sw_load(n)
                if ctx == 2:
                    if not first:
                        wait(sp, d_cq, 2 * g + 9)
                        ctx_load(2 * g + 10, 0)
                    wait(sp, d_cq, 2 * g + (9 if first else 10))
                    ctx_load(2 * g + 11, 1)
                if front:
                    xn_stores(g + 1)
                if first:
                    wait(sp, d_cq, 10)
                    ctx_load(10, 0)
                for j in range(NT):
                    wait(sp, d_out, 4 * g + 2 * j + 2)
                    sp.dma_start(rows(out, g * G + j * P, P), xbuf[r][:, j, :]).then_inc(st_out[r], 16)

            xn_stores(0)
            group(0, 0)
            group(1, 1)
            with sp.Fori(1, 5) as pair:
                group(pair * 2, 0)
                group(pair * 2 + 1, 1)
            for g in range(10, GROUPS - 1):
                group(g, g % 2, ctx=max(12 - g, 0))

            def ew_load(e, m):
                if m < 4:
                    src = rows((w_gate, w_up)[m // 2], e * D + (m % 2) * 512, 512)
                    dst = ew_stage[m].rearrange("p (k i) -> p k i", k=4)
                else:
                    src = rows(w_down, e * I + (m % 2) * 256, 256)
                    dst = ew_stage[m].rearrange("p (k i) -> p k i", k=2)
                sp.dma_start(dst, src.rearrange("(k p) i -> p k i", p=P)).then_inc(ld_ew[m], 16)

            sp.wait_ge(pe_xa, 4 * GROUPS)
            sp.wait_ge(p_xm, 2 * GROUPS)
            for m in range(6):
                ew_load(0, m)
            sp.wait_ge(st_slot, 16 * NT * TOPK * GROUPS)
            with nc.allow_non_contiguous_dma(reason="the slot table is read once"):
                sp.dma_start(tab[:, :, :], slot_dram.rearrange("(c p) w -> p c w", p=HC)).then_inc(ld_tab, 16)
            group(GROUPS - 1, 1, front=False, ctx=0)
            with sp.Fori(1, E) as e:
                for m in range(6):
                    wait(sp, x_lo, e * 6 + (m - 5))
                    ew_load(e, m)
            sp.wait_ge(st_y[0], 16 * E)
            sp.wait_ge(st_y[1], 16 * E)

        @block.gpsimd
        def _(pool):
            gp = nc.gpsimd
            ch = Chain(pool, pool_step)
            ch.do(gp.memset(zeros, 0.0))
            ch.do(gp.iota(slot_init[:, :, 0], [[1, C]], base=T, channel_multiplier=0,
                          allow_small_or_imprecise_dtypes=True))
            ch.do(gp.memset(slot_init[:, :, 1], 0.0))
            ch.do(gp.memset(identf[:, :], 0.0))
            ch.do(gp.memset(tri[:, :], 1.0))
            ch.do(gp.memset(ones[:, :], 1.0))
            ch.do(gp.memset(sel[:, :], 0.0))
            ch.do(gp.memset(expo[:, :], -0.5))
            ch.do(gp.memset(cum[:, :], 0.0))
            ch.do(gp.memset(cumb[:, :], 0.0))
            ch.do(gp.iota(iota_e[:, :], [[1, E]], base=0, channel_multiplier=0, allow_small_or_imprecise_dtypes=True))
            ch.do(gp.iota(tokid[:, :], [[P, NT]], base=0, channel_multiplier=1, allow_small_or_imprecise_dtypes=True))
            ch.sync()
            ch.do(gp.affine_select(out=identf[:, :], in_=identf[:, :], compare_op=ALU.not_equal, fill=1.0, base=0,
                                   pattern=[[-1, P]], channel_multiplier=1))
            ch.do(gp.affine_select(out=tri[:, :], in_=tri[:, :], compare_op=ALU.is_gt, fill=0.0, base=0,
                                   pattern=[[1, P]], channel_multiplier=-1))
            for half in range(2):
                ch.link(gp.affine_select(out=sel[:, :], in_=sel[:, :], compare_op=ALU.not_equal, fill=1.0,
                                         base=-E * half, pattern=[[-1, E]], channel_multiplier=1))
            gp.tensor_copy(identb[:, :], identf[:, :]).then_inc(consts_ready, 2)

            for c in range(XCHUNKS):
                pool.wait_ge(ve1_ready, c + 1)
                gp.tensor_tensor(a1[:, c * CH:(c + 1) * CH], ve1[:, :], expo[:, 0:CH], ALU.pow).then_inc(rs1_ready, 1)
            for n in range(2):
                pool.wait_ge(amax_ready, n + 1)
                gp.partition_all_reduce(sc1[:, 4 * n + 1:4 * n + 2], sc1[:, 4 * n:4 * n + 1], P,
                                        bass.bass_isa.ReduceOp.max).then_inc(amax_all, 1)

            def pool_carry(before):
                wait(pool, p_carry, before)
                carry(gp, 2).then_inc(p_carry, 1)

            def add_mask(f, b):
                pool.wait_ge(ld_mask, 16 * f + 16)
                for j in range(NT):
                    pool.wait_ge(a_v, 2 * f + j + 1)
                    gp.tensor_tensor(xbuf[b][:, j, :], xbuf[b][:, j, :],
                                     mask_first if isinstance(f, int) and f == 0 else mask_sb, ALU.add).then_inc(p_xm, 1)

            def rstd2(f):
                wait(pool, a_xn, 2 * f)
                for j in range(NT):
                    pool.wait_ge(d_var, 2 * f + j + 1)
                    gp.tensor_tensor(rs2[:, j:j + 1], ve2[:, j:j + 1], expo[:, 0:1], ALU.pow).then_inc(p_rs, 1)

            def fill_slots(g):
                pool.wait_ge(d_route, g + 1)
                pool_carry(g)
                for m in range(NT * TOPK):
                    gp.indirect_dma_start(out=slot_dram[:, :],
                                          out_offset=bass.IndirectOffsetOnAxis(ap=dest[:, m:m + 1], axis=0),
                                          in_=payload[:, m, :], in_offset=None,
                                          bounds_check=E * C - 1, oob_is_err=False).then_inc(st_slot, 16)

            add_mask(0, 0)
            rstd2(0)
            pool.wait_ge(st_init, 32)

            def group(g, r, front=True):
                if front:
                    add_mask(g + 1, 1 - r)
                    rstd2(g + 1)
                fill_slots(g)

            group(0, 0)
            group(1, 1)
            with pool.Fori(1, 5) as pair:
                group(pair * 2, 0)
                group(pair * 2 + 1, 1)
            for g in range(10, GROUPS):
                group(g, g % 2, front=g < GROUPS - 1)

            pool.wait_ge(ld_tab, 16)
            ch.do(gp.tensor_scalar(gidx[:, :], tab[:, :, 0], float(T - 1), None, ALU.min))
            ch.do(gp.tensor_copy(sidx[:, :], tab[:, :, 0]))
            ch.do(gp.tensor_scalar(wts[:, :], tab[:, :, 1], DOWN_PROJ, None, ALU.mult))
            ch.sync()
            ch.close()
            SLOT_STEPS = ch.before

            def cols(e):
                return bass.ds(e * 2, 2)

            def gather(e, b, step, carries):
                gp.tensor_copy(gix[:, 2 * b:2 * b + 2], gidx[:, cols(e)]).then_inc(pool_step, 1)
                pool.wait_ge(pool_step, step)
                pool_carry(carries)
                for blk in range(2):
                    gp.indirect_dma_start(out=xg[b][:, blk, :], out_offset=None, in_=xn_dram[:, :],
                                          in_offset=bass.IndirectOffsetOnAxis(ap=gix[:, 2 * b + blk:2 * b + blk + 1],
                                                                              axis=0),
                                          bounds_check=T - 1, oob_is_err=False).then_inc(ld_xg[b], 16)

            def scatter(e, b, step, carries):
                gp.tensor_copy(six[:, 2 * b:2 * b + 2], sidx[:, cols(e)]).then_inc(pool_step, 1)
                pool.wait_ge(pool_step, step)
                pool.wait_ge(x_y, e * 4 + 4)
                pool_carry(carries)
                for blk in range(2):
                    gp.indirect_dma_start(out=out[:, :],
                                          out_offset=bass.IndirectOffsetOnAxis(ap=six[:, 2 * b + blk:2 * b + blk + 1],
                                                                               axis=0),
                                          in_=ybuf[b][:, blk, :], in_offset=None, bounds_check=T + C - 1,
                                          oob_is_err=True, compute_op=ALU.add).then_inc(st_y[b], 16)

            for j in range(NT):
                pool.wait_ge(st_xn[j], 16 * GROUPS)
            pool.wait_ge(pe_xt, 4 * GROUPS)
            gather(0, 0, SLOT_STEPS + 1, GROUPS)
            gather(1, 1, SLOT_STEPS + 2, GROUPS + 1)
            for b in range(2):
                pool.wait_ge(st_out[b], 16 * GROUPS)

            def expert(e, b, more=True):
                if more:
                    steps, carries = e * 2 + (SLOT_STEPS + 2), e * 4 + (GROUPS + 2)
                    pool.wait_ge(x_xt, e * 3 + 3)
                    pool_carry(carries)
                    gather(e + 2, b, steps + 1, carries + 1)
                    steps, carries = steps + 1, carries + 2
                else:
                    steps = SLOT_STEPS + 2 + 2 * (E - 2) + (e - (E - 2))
                    carries = 4 * (E - 2) + GROUPS + 2 + 2 * (e - (E - 2))
                if b == 1:
                    pool.wait_ge(st_y[0], e * 16 + 16)
                else:
                    wait(pool, st_y[1], e * 16)
                pool_carry(carries)
                scatter(e, b, steps + 1, carries + 1)

            expert(0, 0)
            expert(1, 1)
            with pool.Fori(1, E // 2 - 1) as pair:
                expert(pair * 2, 0)
                expert(pair * 2 + 1, 1)
            expert(E - 2, 0, more=False)
            expert(E - 1, 1, more=False)
            for b in range(2):
                pool.wait_ge(st_y[b], 16 * E)

        @block.scalar
        def _(act):
            ac = nc.scalar

            def split_hi(n):
                s, stage = sw_slot(n)
                act.wait_ge(ld_sw[s], 16 * sw_uses(n))
                if n == 0:
                    act.wait_ge(p1_done, XCHUNKS + CCHUNKS)
                if n == 8:
                    act.wait_ge(sw_lo, 8)
                m, k0, k, ih = SW_PIECES[n]
                ac.activation(SW[m][0][:, k0:k0 + k, ih * 512:(ih + 1) * 512],
                              stage.rearrange("p (k i) -> p k i", k=k), ACT.Copy, scale=W_SCALE).then_inc(sw_hi, 1)

            act.dma_start(rw_f, router_t.rearrange("(k p) e -> p k e", p=P)).then_inc(ld_small, 16)
            act.dma_start(bias_sb[:, :], e_bias.partition_broadcast(P)).then_inc(ld_small, 16)
            act.wait_ge(ld_small, 32)
            ac.activation(rw[:, :, 0:E], rw_f, ACT.Copy, scale=W_SCALE).then_inc(rw_hi, 1)

            for c in range(XCHUNKS):
                act.wait_ge(nb1_ready, c + 1)
                for t in range(CH):
                    at = p1_slot[c % 4][:, t * D:(t + 1) * D]
                    n = c * CH + t
                    ins = ac.activation(at, at, ACT.Identity, bias=b1[:, n:n + 1], scale=a1[:, n:n + 1])
                ins.then_inc(ln1_done, 1)

            def x_scaled(f, b):
                settle(act)
                act.wait_ge(ld_x[b], 16 * (f // 2 + 1) if isinstance(f, int) else (f - b) * 8 + 16)
                for j in range(NT):
                    settle(act)
                    wait(act, st_xn[j], 16 * f)
                    wait(act, pe_xt, 4 * f)
                    n = 2 * f + j
                    ac.activation(xn[j], xbuf[b][:, j, :], ACT.Identity, bias=b1[:, bass.ds(n, 1)],
                                  scale=a1[:, bass.ds(n, 1)]).then_inc(a_v, 1)

            def ctx_scaled(view):
                ac.activation(view, view, ACT.Copy, scale=sc1[:, 6:7]).then_inc(a_cv, 1)

            def xq_evac(f):
                wait(act, pe_xa, 4 * f)
                for j in range(NT):
                    act.wait_ge(pe_xq, 2 * f + j + 1)
                    ac.activation(xqT[:, :, j * P:(j + 1) * P],
                                  PS[6 + j][:, :].bitcast(BF16).rearrange("p (k t) -> p k t", k=KD),
                                  ACT.Copy).then_inc(a_xq, 1)

            def ln2(f, b):
                for j in range(NT):
                    act.wait_ge(d_nb, 2 * f + j + 1)
                    ac.activation(xn[j], xbuf[b][:, j, :], ACT.Identity, bias=nb2[:, j:j + 1],
                                  scale=rs2[:, j:j + 1]).then_inc(a_xn, 1)

            def xt_hi(f):
                for j in range(NT):
                    for h in range(2):
                        act.wait_ge(pe_xt, 4 * f + 2 * j + h + 1)
                        ac.activation(xT[0][:, 4 * h:4 * h + 4, j * P:(j + 1) * P],
                                      PS[6 + h][:, :].rearrange("p (k t) -> p k t", k=4), ACT.Copy,
                                      scale=X_SCALE).then_inc(a_xh, 1)

            act.wait_ge(scales_ready, 1)
            act.wait_ge(st_init, 32)
            x_scaled(0, 0)
            xq_evac(0)
            act.wait_ge(scales_ready, 2)
            for m in range(4):
                ctx_scaled(ctx0[m])
            for n in range(4):
                split_hi(n)
            ln2(0, 0)
            xt_hi(0)

            def ring_scaled(slot, count):
                act.wait_ge(ld_ctx[slot], count)
                ctx_scaled(ctx_ring[slot])

            def group(g, r, front=True, ctx=2, weights=None):
                first = isinstance(g, int) and g == 0
                for ic in range(KS):
                    if first:
                        for n in FIRST_SPLITS[ic]:
                            split_hi(n)
                    act.wait_ge(pe_gu, 8 * g + ic + 1)
                    wait(act, d_t, 8 * g + (ic - 1 if ic > 1 else 0))
                    ac.activation(sig[ic % 2], PS[ic % 2][:, 0:G], ACT.Sigmoid, scale=UP_PROJ).then_inc(a_sig, 1)
                    act.wait_ge(d_h, 8 * g + ic + 1)
                    if ic == 0:
                        wait(act, pe_dn, 4 * g)
                    ac.activation(hT[0][:, ic, :], h32[ic % 2], ACT.Copy).then_inc(a_hh, 1)
                    if ic == 0:
                        act.wait_ge(pe_lg, g + 1)
                        ac.activation(lg[:, :], logit_ps, ACT.Copy, scale=UP_PROJ).then_inc(a_lg, 1)
                    if ic == 1:
                        act.wait_ge(pe_lt, g + 1)
                        wait(act, d_route, g)
                        ac.activation(s_sb[:, :, :], score_ps.rearrange("p (t e) -> p t e", t=NT),
                                      ACT.Sigmoid).then_inc(a_sc, 1)
                        if front:
                            x_scaled(g + 1, 1 - r)
                    if ctx and ic == 3:
                        ring_scaled(1, 16 * g + 16)
                    if ctx == 2 and ic == 5:
                        ring_scaled(0, 16 if first else 16 * g + 32)
                    if front and ic == 6:
                        xq_evac(g + 1)
                if weights:
                    weights()
                if first:
                    for n in FIRST_SPLITS[KS]:
                        split_hi(n)
                if front:
                    ln2(g + 1, 1 - r)
                    xt_hi(g + 1)
                if first:
                    ring_scaled(0, 32)

            act.wait_ge(rw_lo, 1)
            group(0, 0)
            group(1, 1)
            with act.Fori(1, 5) as pair:
                group(pair * 2, 0)
                group(pair * 2 + 1, 1)
            for g in range(10, GROUPS - 1):
                group(g, g % 2, ctx=max(12 - g, 0))

            def ew_hi(e, b, m, first=False):
                act.wait_ge(ld_ew[m], e * 16 + 16)
                if first and m == 0:
                    act.wait_ge(pe_gu, 8 * GROUPS)
                if not first:
                    wait(act, x_gu if m < 4 else x_dn, e * 4 - 4)
                stage = ew_stage[m]
                if m < 4:
                    dst = EW[b][m // 2][0][:, (m % 2) * 4:(m % 2) * 4 + 4, :]
                    stage = stage.rearrange("p (k i) -> p k i", k=4)
                else:
                    dst = EW[b][2][0][:, (m % 2) * 2:(m % 2) * 2 + 2, :]
                    stage = stage.rearrange("p (k i) -> p k i", k=2)
                ac.activation(dst, stage, ACT.Copy, scale=W_SCALE).then_inc(x_hi, 1)

            def et_hi(e):
                for s in range(3):
                    k = 3 if s < 2 else 2
                    act.wait_ge(x_xt, e * 3 + (s + 1))
                    ac.activation(eT[0][:, 3 * s:3 * s + k, :],
                                  PS[(2, 3, 6)[s]][:, 0:k * C].rearrange("p (k t) -> p k t", k=k), ACT.Copy,
                                  scale=X_SCALE).then_inc(x_xh, 1)

            group(GROUPS - 1, 1, front=False, ctx=0,
                  weights=lambda: [ew_hi(0, 0, m, first=True) for m in range(6)])
            et_hi(0)
            act.wait_ge(pe_dn, 4 * GROUPS)
            for b in range(2):
                act.wait_ge(st_out[b], 16 * GROUPS)

            def product_out(e, q):
                act.wait_ge(x_dn, e * 4 + (q + 1))
                wait(act, x_tr, e * 4)
                ac.activation(yT[q // 2][:, 2 * (q % 2):2 * (q % 2) + 2, :],
                              PS[DOWN_BANKS[q]][:, 0:2 * C].rearrange("p (k t) -> p k t", k=2),
                              ACT.Copy).then_inc(x_yt, 1)

            def rows_out(e, b, u):
                hf, blk = u // 2, u % 2
                settle(act)
                if u == 0:
                    wait(act, st_y[b], (e - b) * 16)
                act.wait_ge(x_tr, e * 4 + (u + 1))
                ac.activation(ybuf[b][:, blk, hf * HALF:(hf + 1) * HALF], PS[ROW_BANKS[u]][0:HC, :], ACT.Copy,
                              scale=wts[:, bass.ds(e * 2 + blk, 1)]).then_inc(x_y, 1)

            def expert(e, b, before=True, more=True):
                for ic in range(KI):
                    act.wait_ge(x_gu, e * 4 + (ic + 1))
                    wait(act, x_t, e * 4 + (ic - 1 if ic > 1 else 0))
                    ac.activation(sig[ic % 2][:, 0:C], PS[ic % 2][:, 0:C], ACT.Sigmoid, scale=UP_PROJ).then_inc(x_sig, 1)
                    act.wait_ge(x_h, e * 4 + (ic + 1))
                    if ic == 0:
                        wait(act, x_dn, e * 4)
                    ac.activation(ehT[0][:, ic, :], h32[ic % 2][:, 0:C], ACT.Copy).then_inc(x_hh, 1)
                    if ic == 0 and before:
                        for u in (2, 3):
                            rows_out(e - 1, 1 - b, u)
                    if more and ic < 3:
                        ew_hi(e + 1, 1 - b, ic)
                if more:
                    et_hi(e + 1)
                    ew_hi(e + 1, 1 - b, 3)
                product_out(e, 0)
                product_out(e, 1)
                product_out(e, 2)
                if more:
                    ew_hi(e + 1, 1 - b, 4)
                product_out(e, 3)
                for u in (0, 1):
                    rows_out(e, b, u)
                if more:
                    ew_hi(e + 1, 1 - b, 5)
                else:
                    for u in (2, 3):
                        rows_out(e, b, u)

            expert(0, 0, before=False)
            expert(1, 1)
            with act.Fori(1, E // 2 - 1) as pair:
                expert(pair * 2, 0)
                expert(pair * 2 + 1, 1)
            expert(E - 2, 0)
            expert(E - 1, 1, more=False)

        @block.vector
        def _(dve):
            ve = nc.vector
            ch = Chain(dve, d_chain)

            dve.wait_ge(consts_ready, 2)

            def abs_max(view, col):
                ins = ve.tensor_reduce(amax[:, col:col + 1], view, AX.X, ALU.max, apply_absolute_value=True)
                return ins

            def x_abs_max(c):
                dve.wait_ge(ln1_done, c + 1)
                abs_max(p1_slot[c % 4], c).then_inc(p1_done, 1)

            for c in range(XCHUNKS):
                if c > 1:
                    dve.wait_ge(ld_p1[c % 4], 16 * p1_loads(c))
                for t in range(CH):
                    if c < 2:
                        dve.wait_ge(ld_first[c * CH + t], 16)
                    for h in range(2):
                        ch.do(ve.bn_stats(st1[:, t, h, :], p1_slot[c % 4][:, t * D + h * HALF:t * D + (h + 1) * HALF]))
                ch.sync()
                for t in range(CH):
                    ch.do(ve.bn_aggr(mv1[:, t, :], st1[:, t, :, :]))
                ch.sync()
                ve.tensor_scalar(ve1[:, :], mv1[:, :, 1], LN_EPS, None, ALU.add).then_inc(ve1_ready, 1)
                if c == 0:
                    dve.wait_ge(rw_hi, 1)
                    ve.scalar_tensor_tensor(out=rw[:, :, E:2 * E], in0=rw_f, scalar=W_SCALE, in1=rw[:, :, 0:E],
                                            op0=ALU.mult, op1=ALU.subtract).then_inc(rw_lo, 1)
                if c:
                    x_abs_max(c - 1)
                dve.wait_ge(rs1_ready, c + 1)
                ve.scalar_tensor_tensor(out=b1[:, c * CH:(c + 1) * CH], in0=mv1[:, :, 0], scalar=-1.0,
                                        in1=a1[:, c * CH:(c + 1) * CH], op0=ALU.mult, op1=ALU.mult).then_inc(nb1_ready, 1)
            dve.wait_ge(ld_p1[XCHUNKS % 4], 16 * p1_loads(XCHUNKS))
            ch.do(abs_max(p1_slot[XCHUNKS % 4], XCHUNKS))
            dve.wait_ge(ln1_done, XCHUNKS)
            abs_max(p1_slot[(XCHUNKS - 1) % 4], XCHUNKS - 1).then_inc(p1_done, 2)
            dve.wait_ge(p1_done, XCHUNKS + 1)
            ve.tensor_reduce(sc1[:, 0:1], amax[:, 0:XCHUNKS], AX.X, ALU.max).then_inc(amax_ready, 1)

            def ctx_abs_max(c):
                dve.wait_ge(ld_p1[c % 4], 16 * p1_loads(c))
                abs_max(p1_slot[c % 4], c).then_inc(p1_done, 1)

            def fp8_scale(n):
                at = 4 * n
                dve.wait_ge(amax_all, n + 1)
                ch.link(ve.tensor_scalar(sc1[:, at + 1:at + 2], sc1[:, at + 1:at + 2], 1e-12, None, ALU.max))
                ch.link(ve.reciprocal(sc1[:, at + 3:at + 4], sc1[:, at + 1:at + 2]))
                ch.link(ve.tensor_scalar(sc1[:, at + 2:at + 3], sc1[:, at + 3:at + 4], FP8_MAX, None, ALU.mult))
                ch.link(ve.reciprocal(sc1[:, at + 3:at + 4], sc1[:, at + 2:at + 3]))

            def fp8_round(v, scratch, dst):
                ch.link(ve.tensor_scalar(v, v, FP8_MAX, -FP8_MAX, ALU.min, ALU.max))
                ch.link(ve.tensor_scalar(scratch.bitcast(I32), v.bitcast(I32), EXPONENT_BITS, None, ALU.bitwise_and))
                ch.link(ve.tensor_scalar(scratch, scratch, FP8_MIN_NORMAL, ROUNDER, ALU.max, ALU.mult))
                ch.link(ve.tensor_tensor(v, v, scratch, ALU.add))
                return ve.tensor_tensor(dst, v, scratch, ALU.subtract)

            def x_round(f, j, scratch):
                dve.wait_ge(a_v, 2 * f + j + 1)
                wait(dve, pe_xq, 2 * f)
                fp8_round(xn[j], scratch, xq[j]).then_inc(d_q, 1)

            ctx_abs_max(XCHUNKS + 1)
            fp8_scale(0)
            ch.do(ve.tensor_scalar(a1[:, :], a1[:, :], sc1[:, 2:3], None, ALU.mult))
            ch.do(ve.tensor_scalar(b1[:, :], b1[:, :], sc1[:, 2:3], None, ALU.mult))
            ch.sync()
            ve.tensor_copy(sc1[:, 8:9], sc1[:, 2:3]).then_inc(scales_ready, 1)
            ctx_abs_max(XCHUNKS + 2)
            for j in range(NT):
                x_round(0, j, M_first[:, 0:D])
            for c in range(XCHUNKS + 3, XCHUNKS + CCHUNKS):
                ctx_abs_max(c)
            for m in range(4):
                dve.wait_ge(ld_c0[m], 16)
                ch.do(abs_max(ctx0[m], XCHUNKS + CCHUNKS + m))
            ch.sync()
            dve.wait_ge(p1_done, XCHUNKS + CCHUNKS)
            ve.tensor_reduce(sc1[:, 4:5], amax[:, XCHUNKS:], AX.X, ALU.max).then_inc(amax_ready, 1)
            fp8_scale(1)
            ve.tensor_tensor(sc1[:, 9:10], sc1[:, 3:4], sc1[:, 7:8], ALU.mult).then_inc(scales_ready, 1)

            dve.wait_ge(scales_ready, 2)
            for m in range(4):
                dve.wait_ge(a_cv, m + 1)
                fp8_round(ctx0[m], M_first, BIG[:, 2 * m * D:2 * (m + 1) * D]).then_inc(d_cq, 2)

            def split_lo(n):
                s, stage = sw_slot(n)
                m, k0, k, ih = SW_PIECES[n]
                dve.wait_ge(sw_hi, n + 1)
                cut = (slice(None), slice(k0, k0 + k), slice(ih * 512, (ih + 1) * 512))
                ve.scalar_tensor_tensor(out=SW[m][1][cut], in0=stage.rearrange("p (k i) -> p k i", k=k),
                                        scalar=W_SCALE, in1=SW[m][0][cut], op0=ALU.mult,
                                        op1=ALU.subtract).then_inc(sw_lo, 1)

            def residual(f, b):
                for j in range(NT):
                    dve.wait_ge(p_xm, 2 * f + j + 1)
                    for h in range(2):
                        at = xbuf[b][:, j, h * HALF:(h + 1) * HALF]
                        dve.wait_ge(pe_xa, 4 * f + 2 * j + h + 1)
                        bank = PS[4 + h] if j and isinstance(f, int) and f == 0 else PS[2 + h]
                        ve.scalar_tensor_tensor(out=at, in0=bank[:, :], scalar=sc1[:, 9:10], in1=at,
                                                op0=ALU.mult, op1=ALU.add).then_inc(d_x2, 1)
                    dve.wait_ge(d_x2, 4 * f + 2 * j + 2)
                    for h in range(2):
                        ch.do(ve.bn_stats(st2[:, j, h, :], xbuf[b][:, j, h * HALF:(h + 1) * HALF]))
                    ch.sync()
                    carry(ve, 1)
                    ch.link(ve.bn_aggr(mv2[:, j, :], st2[:, j, :, :]))
                    ve.tensor_scalar(ve2[:, j:j + 1], mv2[:, j, 1:2], LN_EPS, None, ALU.add).then_inc(d_var, 1)

            def shift(f):
                for j in range(NT):
                    dve.wait_ge(p_rs, 2 * f + j + 1)
                    ve.scalar_tensor_tensor(out=nb2[:, j:j + 1], in0=mv2[:, j, 0:1], scalar=-1.0, in1=rs2[:, j:j + 1],
                                            op0=ALU.mult, op1=ALU.mult).then_inc(d_nb, 1)

            def xt_lo(f, j):
                for h in range(2):
                    dve.wait_ge(a_xh, 4 * f + 2 * j + h + 1)
                    ve.scalar_tensor_tensor(out=xT[1][:, 4 * h:4 * h + 4, j * P:(j + 1) * P],
                                            in0=PS[6 + h][:, :].rearrange("p (k t) -> p k t", k=4), scalar=X_SCALE,
                                            in1=xT[0][:, 4 * h:4 * h + 4, j * P:(j + 1) * P],
                                            op0=ALU.mult, op1=ALU.subtract).then_inc(d_xl, 1)

            residual(0, 0)
            split_lo(0)
            shift(0)
            split_lo(1)
            xt_lo(0, 0)
            xt_lo(0, 1)
            for n in range(2, 4):
                split_lo(n)

            def route_picks(g):
                dve.wait_ge(a_sc, g + 1)
                ch.link(ve.tensor_tensor(sc[:, :, :], s_sb[:, :, :], bias_sb[:, :].unsqueeze(1).to_broadcast([P, NT, E]),
                                         ALU.add))
                q = sc[:, :, :].rearrange("p t (g i) -> p (t g) i", i=EPG)
                ch.do(ve.tensor_tensor(g_a[:, :], q[:, :, 0], q[:, :, 1], ALU.max))
                ch.do(ve.tensor_tensor(g_b[:, :], q[:, :, 2], q[:, :, 3], ALU.max))
                ch.do(ve.tensor_tensor(g_c[:, :], q[:, :, 0], q[:, :, 1], ALU.add))
                ch.do(ve.tensor_tensor(g_d[:, :], q[:, :, 2], q[:, :, 3], ALU.add))
                ch.sync()
                ch.do(ve.tensor_tensor(g_a[:, :], g_a[:, :], g_b[:, :], ALU.add))
                ch.do(ve.tensor_tensor(g_c[:, :], g_c[:, :], g_d[:, :], ALU.max))
                ch.sync()
                ch.do(ve.tensor_tensor(g_a[:, :], g_a[:, :], g_c[:, :], ALU.max))
                ga = g_a[:, :].rearrange("p (t g) -> p t g", t=NT)
                ch.sync()
                carry(ve, 1)
                for j in range(NT):
                    ch.do(ve.max(g_top[:, j, :], ga[:, j, :]))
                ch.sync()
                carry(ve, 1)
                for j in range(NT):
                    ch.do(ve.max_index(g_idx[:, j, :], g_top[:, j, :], ga[:, j, :]))
                ch.sync()
                ch.link(ve.tensor_copy(g_idf[:, :, :], g_idx[:, :, :]))
                ch.link(ve.tensor_tensor(g_eq[:, :, :, :],
                                         iota_e[:, 0:NGRP].unsqueeze(1).unsqueeze(1).to_broadcast([P, NT, TOPG, NGRP]),
                                         g_idf[:, :, 0:TOPG].unsqueeze(3).to_broadcast([P, NT, TOPG, NGRP]),
                                         ALU.is_equal))
                ch.link(ve.tensor_reduce(g_b[:, :].rearrange("p (t g) -> p t g", t=NT),
                                         g_eq[:, :, :, :].rearrange("p t k g -> p t g k"), AX.X, ALU.add))
                ch.link(ve.tensor_tensor(masked[:, :, :].rearrange("p t (g i) -> p (t g) i", i=EPG), q,
                                         g_b[:, :].unsqueeze(2).to_broadcast([P, NT * NGRP, EPG]), ALU.mult))
                ch.do(ve.tensor_scalar(masked[:, :, :], masked[:, :, :], 0.0, None, ALU.add))
                ch.sync()
                carry(ve, 1)
                for j in range(NT):
                    ch.do(ve.max(e_top[:, j, :], masked[:, j, :]))
                ch.sync()
                carry(ve, 1)
                for j in range(NT):
                    ch.do(ve.max_index(e_idx[:, j, :], e_top[:, j, :], masked[:, j, :]))
                ch.sync()
                ch.link(ve.tensor_copy(e_idf[:, :, :], e_idx[:, :, 0:TOPK]))
                ch.link(ve.tensor_tensor(e_eq[:, :, :, :],
                                         iota_e[:, :].unsqueeze(1).unsqueeze(1).to_broadcast([P, NT, TOPK, E]),
                                         e_idf[:, :, :].unsqueeze(3).to_broadcast([P, NT, TOPK, E]), ALU.is_equal))
                with nc.allow_low_precision(reason="zeros and ones"):
                    ve.tensor_reduce(picks[:, :, :], e_eq[:, :, :, :].rearrange("p t k e -> p t e k"), AX.X,
                                     ALU.add).then_inc(d_picks, 1)
                ch.link(ve.tensor_tensor(e_pr[:, :, :, :], e_eq[:, :, :, :],
                                         s_sb[:, :, :].unsqueeze(2).to_broadcast([P, NT, TOPK, E]), ALU.mult))
                ch.link(ve.tensor_reduce(r_w[:, :, :], e_pr[:, :, :, :], AX.X, ALU.add))
                ch.link(ve.tensor_reduce(r_den[:, :], r_w[:, :, :], AX.X, ALU.add))
                ch.link(ve.tensor_scalar(r_den[:, :], r_den[:, :], 1e-20, None, ALU.add))
                ch.link(ve.reciprocal(r_den[:, :], r_den[:, :]))
                ch.link(ve.tensor_tensor(r_w[:, :, :], r_w[:, :, :], r_den[:, :].unsqueeze(2).to_broadcast([P, NT, TOPK]),
                                         ALU.mult))

            def route_slots(g):
                dve.wait_ge(pe_pos, g + 1)
                ch.link(ve.tensor_tensor(e_pr[:, :, :, :], e_eq[:, :, :, :],
                                         pos_ps.unsqueeze(2).to_broadcast([P, NT, TOPK, E]), ALU.mult))
                ch.link(ve.tensor_reduce(r_pos[:, :, :], e_pr[:, :, :, :], AX.X, ALU.add))
                ch.do(ve.tensor_scalar(r_ge[:, :, :], r_pos[:, :, :], float(C), NO_SLOT, ALU.is_ge, ALU.mult))
                ch.do(ve.scalar_tensor_tensor(out=r_pos[:, :, :], in0=e_idf[:, :, :], scalar=float(C),
                                              in1=r_pos[:, :, :], op0=ALU.mult, op1=ALU.add))
                ch.do(ve.tensor_tensor(cum[:, :], cum[:, :], picks[:, 0, :], ALU.add))
                ch.sync()
                wait(dve, st_slot, g * (16 * NT * TOPK))
                ch.do(ve.tensor_tensor(dest[:, :].rearrange("p (t k) -> p t k", t=NT), r_pos[:, :, :], r_ge[:, :, :],
                                       ALU.add))
                ch.do(ve.tensor_scalar(payload[:, :, 1].rearrange("p (t k) -> p t k", t=NT), r_w[:, :, :],
                                       ROUTED_SCALE, None, ALU.mult))
                ch.do(ve.tensor_copy(payload[:, :, 0].rearrange("p (t k) -> p t k", t=NT),
                                     tokid[:, :].unsqueeze(2).to_broadcast([P, NT, TOPK])))
                ch.link(ve.tensor_tensor(cum[:, :], cum[:, :], picks[:, 1, :], ALU.add))
                ch.do(ve.tensor_scalar(tokid[:, :], tokid[:, :], float(G), None, ALU.add))
                ch.do(ve.tensor_copy(cumb[:, :], cum[:, :]))
                ch.sync()
                ve.tensor_copy(sc1[:, 10:11], sc1[:, 9:10]).then_inc(d_route, 1)

            def add_shared(g, r, u):
                j, h = u // 2, u % 2
                at = xbuf[r][:, j, h * HALF:(h + 1) * HALF]
                dve.wait_ge(pe_dn, 4 * g + u + 1)
                ve.scalar_tensor_tensor(out=at, in0=PS[4 + u % 2][:, :], scalar=DOWN_PROJ, in1=at, op0=ALU.mult,
                                        op1=ALU.add).then_inc(d_out, 1)

            def ctx_round(g, t, slot, tiles):
                dve.wait_ge(a_cv, tiles - 4)
                wait(dve, pe_xa, 4 * g + 4)
                fp8_round(ctx_ring[slot], M_main, BIG[:, bass.ds((t & 15) * D, D)]).then_inc(d_cq, 1)

            def group(g, r, front=True, ctx=2, weights=None):
                first = isinstance(g, int) and g == 0
                for ic in range(KS):
                    if first:
                        for n in FIRST_SPLITS[ic]:
                            split_lo(n)
                    n = 8 * g + ic
                    bank = PS[ic % 2]
                    dve.wait_ge(a_sig, n + 1)
                    ve.scalar_tensor_tensor(out=gup, in0=bank[:, G:2 * G], scalar=H_SCALE * UP_PROJ * UP_PROJ,
                                            in1=sig[ic % 2], op0=ALU.mult, op1=ALU.mult).then_inc(d_t, 1)
                    dve.wait_ge(d_t, n + 1)
                    wait(dve, a_hh, 8 * g + (ic - 1 if ic > 1 else 0))
                    ve.tensor_tensor(h32[ic % 2], gup, bank[:, 0:G], ALU.mult).then_inc(d_h, 1)
                    if ic == 1:
                        route_picks(g)
                    if front and ic - first in (2, 3):
                        x_round(g + 1, ic - first - 2, M_main)
                    if ctx and ic - first == 4:
                        ctx_round(g, 2 * g + 9, 1, 2 * g + 10)
                    if ic == 6:
                        route_slots(g)
                    dve.wait_ge(a_hh, n + 1)
                    ve.tensor_tensor(hT[1][:, ic, :], h32[ic % 2], hT[0][:, ic, :], ALU.subtract).then_inc(d_hl, 1)
                if front:
                    residual(g + 1, 1 - r)
                    shift(g + 1)
                if first:
                    for n in FIRST_SPLITS[KS]:
                        split_lo(n)
                if weights:
                    weights(0)
                add_shared(g, r, 0)
                if ctx == 2:
                    if first:
                        ctx_round(0, 8, 0, 10)
                    else:
                        ctx_round(g, 2 * g + 10, 0, 2 * g + 11)
                if weights:
                    weights(1)
                add_shared(g, r, 1)
                if front:
                    xt_lo(g + 1, 0)
                if weights:
                    weights(2)
                add_shared(g, r, 2)
                if front:
                    xt_lo(g + 1, 1)
                if weights:
                    weights(3)
                add_shared(g, r, 3)
                if first:
                    ctx_round(0, 10, 0, 11)

            ch.close()
            STEPS = GROUP_STEPS
            group(0, 0)
            group(1, 1)
            ch.close()
            base = ch.before - 2 * STEPS
            with dve.Fori(1, 5) as pair:
                for r in range(2):
                    ch.before, ch.n = pair * (2 * STEPS) + (base + r * STEPS), 0
                    group(pair * 2 + r, r)
                    assert ch.n == STEPS, ch.n
            ch.before, ch.n = base + 10 * STEPS, 0

            def ew_lo(e, b, m):
                dve.wait_ge(x_hi, e * 6 + (m + 1))
                stage = ew_stage[m]
                k = 4 if m < 4 else 2
                src = stage.rearrange("p (k i) -> p k i", k=k)
                cut = (slice(None), slice((m % 2) * k, (m % 2) * k + k), slice(None))
                hi, lo = EW[b][m // 2]
                ve.scalar_tensor_tensor(out=lo[cut], in0=src, scalar=W_SCALE, in1=hi[cut], op0=ALU.mult,
                                        op1=ALU.subtract).then_inc(x_lo, 1)

            def et_lo(e):
                for s in range(3):
                    k = 3 if s < 2 else 2
                    dve.wait_ge(x_xh, e * 3 + (s + 1))
                    ve.scalar_tensor_tensor(out=eT[1][:, 3 * s:3 * s + k, :],
                                            in0=PS[(2, 3, 6)[s]][:, 0:k * C].rearrange("p (k t) -> p k t", k=k),
                                            scalar=X_SCALE, in1=eT[0][:, 3 * s:3 * s + k, :], op0=ALU.mult,
                                            op1=ALU.subtract).then_inc(x_xl, 1)

            for g in range(10, GROUPS):
                last = g == GROUPS - 1
                group(g, g % 2, front=not last, ctx=max(12 - g, 0),
                      weights=(lambda n: ew_lo(0, 0, n)) if last else None)
            ew_lo(0, 0, 4)
            et_lo(0)

            def expert(e, b, more=True):
                for ic in range(KI):
                    bank = PS[ic % 2]
                    dve.wait_ge(x_sig, e * 4 + (ic + 1))
                    ve.scalar_tensor_tensor(out=gup[:, 0:C], in0=bank[:, G:G + C], scalar=H_SCALE * UP_PROJ * UP_PROJ,
                                            in1=sig[ic % 2][:, 0:C], op0=ALU.mult, op1=ALU.mult).then_inc(x_t, 1)
                    dve.wait_ge(x_t, e * 4 + (ic + 1))
                    wait(dve, x_hh, e * 4 + (ic - 1 if ic > 1 else 0))
                    ve.tensor_tensor(h32[ic % 2][:, 0:C], gup[:, 0:C], bank[:, 0:C], ALU.mult).then_inc(x_h, 1)
                    dve.wait_ge(x_hh, e * 4 + (ic + 1))
                    ve.tensor_tensor(ehT[1][:, ic, :], h32[ic % 2][:, 0:C], ehT[0][:, ic, :],
                                     ALU.subtract).then_inc(x_hl, 1)
                    if ic == 0:
                        ew_lo(e, b, 5)
                    elif more and ic < 3:
                        ew_lo(e + 1, 1 - b, ic - 1)
                if more:
                    et_lo(e + 1)
                    for m in range(2, 5):
                        ew_lo(e + 1, 1 - b, m)

            expert(0, 0)
            expert(1, 1)
            with dve.Fori(1, E // 2 - 1) as pair:
                expert(pair * 2, 0)
                expert(pair * 2 + 1, 1)
            expert(E - 2, 0)
            expert(E - 1, 1, more=False)

        @block.tensor
        def _(pe):
            te = nc.tensor

            def product(out_ps, weights, data, chunks, cols, pieces=None):
                (whi, wlo), (xhi, xlo) = weights, data
                steps = [(a, b, k) for k in range(chunks) for a, b in ((whi, xhi), (whi, xlo), (wlo, xhi))]
                for n, (a, b, k) in enumerate(steps):
                    if pieces is not None and n in (0, len(steps) // 2):
                        pe.wait_ge(sw_lo, pieces + 1 + (n > 0))
                    ins = te.matmul(out_ps, a[:, k, cols], b[:, k, :], start=n == 0, stop=n == len(steps) - 1)
                return ins

            def down(out_ps, acts, weights, chunks, toks, cols, last_chunk=None):
                (hhi, hlo), (whi, wlo) = acts, weights
                steps = [(a, b, k) for k in range(chunks) for a, b in ((hhi, whi), (hhi, wlo), (hlo, whi))]
                for n, (a, b, k) in enumerate(steps):
                    if last_chunk and n == 3 * (chunks - 1):
                        pe.wait_ge(*last_chunk)
                    ins = te.matmul(out_ps, a[:, k, toks], b[:, k, cols], start=n == 0, stop=n == len(steps) - 1)
                return ins

            def xq_transpose(f):
                wait(pe, d_xl, 4 * f)
                for j in range(NT):
                    pe.wait_ge(d_q, 2 * f + j + 1)
                    bank = PS[6 + j][:, :].bitcast(BF16)
                    for k in range(KD):
                        ins = te.transpose(bank[:, k * P:(k + 1) * P], xq[j][:, k * P:(k + 1) * P], identb[:, :])
                    ins.then_inc(pe_xq, 1)

            def cross(f):
                batch = f >> 2
                pe.wait_ge(d_cq, batch * 8 + 8)
                wait(pe, a_lg, f)
                wait(pe, d_route, f)
                for j in range(NT):
                    pe.wait_ge(a_xq, 2 * f + j + 1)
                    for h in range(2):
                        if j:
                            pe.wait_ge(d_x2, 4 * f + h + 1)
                        for k in range(KD):
                            ctx_at = (batch & 1) * (8 * D) + (k * D + h * HALF)
                            ins = te.matmul(PS[2 + h][:, :], xqT[:, k, j * P:(j + 1) * P], BIG[:, bass.ds(ctx_at, HALF)],
                                            start=k == 0, stop=k == KD - 1)
                        ins.then_inc(pe_xa, 1)

            def cross_first():
                pe.wait_ge(a_xq, 2)
                for k in range(KD):
                    if k % 2 == 0:
                        pe.wait_ge(d_cq, k + 2)
                    for j in range(NT):
                        for h in range(2):
                            ins = te.matmul(PS[2 + 2 * j + h][:, :], xqT[:, k, j * P:(j + 1) * P],
                                            BIG[:, k * D + h * HALF:k * D + (h + 1) * HALF],
                                            start=k == 0, stop=k == KD - 1)
                            if k == KD - 1:
                                ins.then_inc(pe_xa, 1)

            def xt_transpose(f, j):
                pe.wait_ge(a_xn, 2 * f + j + 1)
                for h in range(2):
                    if j == 0:
                        pe.wait_ge(a_xq, 2 * f + h + 1)
                    else:
                        pe.wait_ge(d_xl, 4 * f + h + 1)
                    for k in range(4):
                        ins = te.transpose(PS[6 + h][:, k * P:(k + 1) * P], xn[j][:, (4 * h + k) * P:(4 * h + k + 1) * P],
                                           identf[:, :])
                    ins.then_inc(pe_xt, 1)

            def group(g, r, front=True):
                pe.wait_ge(d_xl, 4 * g + 4)
                for ic in range(KS):
                    first = isinstance(g, int) and g == 0 and ic % 4 == 0
                    wait(pe, d_h, 8 * g + (ic - 1 if ic > 1 else 0))
                    cols = slice(ic * P, (ic + 1) * P)
                    product(PS[ic % 2][:, 0:G], SW[0], xT, KD, cols, ic if first else None)
                    product(PS[ic % 2][:, G:2 * G], SW[1], xT, KD, cols, ic + 2 if first else None).then_inc(pe_gu, 1)
                    if ic == 0:
                        pe.wait_ge(d_x2, 4 * g + 4)
                        for k in range(KD):
                            for v in range(2):
                                ins = te.matmul(logit_ps, rw[:, k, :], xT[v][:, k, :], start=k + v == 0,
                                                stop=k == KD - 1 and v == 1)
                        ins.then_inc(pe_lg, 1)
                    if ic == 1:
                        pe.wait_ge(a_lg, g + 1)
                        for j in range(NT):
                            ins = te.matmul(score_ps[:, j * E:(j + 1) * E], lg[:, j * P:(j + 1) * P], sel[:, :],
                                            start=True, stop=True)
                        ins.then_inc(pe_lt, 1)
                    if ic == 5:
                        pe.wait_ge(d_picks, g + 1)
                        pe.wait_ge(a_sc, g + 1)
                        wait(pe, d_route, g)
                        te.matmul(pos_ps[:, 0, :], tri[:, :], picks[:, 0, :], start=True, stop=False)
                        te.matmul(pos_ps[:, 0, :], ones[:, :], cumb[:, :], start=False, stop=True)
                        te.matmul(pos_ps[:, 1, :], tri[:, :], picks[:, 1, :], start=True, stop=False)
                        te.matmul(pos_ps[:, 1, :], ones[:, :], picks[:, 0, :], start=False, stop=False)
                        te.matmul(pos_ps[:, 1, :], ones[:, :], cumb[:, :], start=False, stop=True).then_inc(pe_pos, 1)
                    if front and ic == 6:
                        xq_transpose(g + 1)
                if front:
                    cross(g + 1)
                pe.wait_ge(d_hl, 8 * g + 7)
                for u in range(4):
                    j, h = u // 2, u % 2
                    wait(pe, d_out, 4 * g + (u - 1 if u > 1 else 0))
                    if front and u in (2, 3):
                        xt_transpose(g + 1, u - 2)
                    if isinstance(g, int) and g == 0 and u < 2:
                        pe.wait_ge(sw_lo, 12 + 4 * u)
                    down(PS[4 + u % 2][:, :], hT, SW[2], KS, slice(j * P, (j + 1) * P),
                         slice(h * HALF, (h + 1) * HALF),
                         last_chunk=(d_hl, 8 * g + 8) if u == 0 else None).then_inc(pe_dn, 1)

            pe.wait_ge(consts_ready, 2)
            xq_transpose(0)
            cross_first()
            xt_transpose(0, 0)
            xt_transpose(0, 1)
            pe.wait_ge(rw_lo, 1)
            group(0, 0)
            group(1, 1)
            with pe.Fori(1, 5) as pair:
                group(pair * 2, 0)
                group(pair * 2 + 1, 1)
            for g in range(10, GROUPS):
                group(g, g % 2, front=g < GROUPS - 1)

            def et_transpose(e, b):
                pe.wait_ge(ld_xg[b], (e - b) * 16 + 32)
                for s in range(3):
                    for k in range(3 if s < 2 else 2):
                        for blk in range(2):
                            kk = 3 * s + k
                            ins = te.transpose(PS[(2, 3, 6)[s]][:, k * C + blk * HC:k * C + (blk + 1) * HC],
                                               xg[b][:, blk, kk * P:(kk + 1) * P], identf[0:HC, 0:HC])
                    ins.then_inc(x_xt, 1)

            pe.wait_ge(a_lg, GROUPS)
            pe.wait_ge(d_route, GROUPS)
            et_transpose(0, 0)
            pe.wait_ge(d_h, 8 * GROUPS)
            pe.wait_ge(d_out, 4 * GROUPS)

            def rows_transpose(e, hf, after=None):
                pe.wait_ge(x_yt, e * 4 + (2 * hf + 2))
                for blk in range(2):
                    u = 2 * hf + blk
                    if u < 3:
                        pe.wait_ge(x_xl, after * 3 + (u + 1))
                    for k in range(4):
                        ins = te.transpose(PS[ROW_BANKS[u]][0:HC, k * P:(k + 1) * P],
                                           yT[hf][:, k, blk * HC:(blk + 1) * HC], identf[:, :])
                    ins.then_inc(x_tr, 1)

            def expert(e, b, before=True, more=True):
                pe.wait_ge(x_lo, e * 6 + 4)
                pe.wait_ge(x_xl, e * 3 + 3)
                for ic in range(KI):
                    wait(pe, x_h, e * 4 + (ic - 1 if ic > 1 else 0))
                    cols = slice(ic * P, (ic + 1) * P)
                    product(PS[ic % 2][:, 0:C], EW[b][0], eT, KD, cols)
                    product(PS[ic % 2][:, G:G + C], EW[b][1], eT, KD, cols).then_inc(x_gu, 1)
                    if ic == 0 and before:
                        rows_transpose(e - 1, 1, after=e)
                wait(pe, x_y, e * 4)
                if more:
                    et_transpose(e + 1, 1 - b)
                pe.wait_ge(x_lo, e * 6 + 6)
                pe.wait_ge(x_hl, e * 4 + 3)
                (whi, wlo), (hhi, hlo) = EW[b][2], ehT
                for n, (q, c, k) in enumerate(DOWN_ORDER):
                    if n == DOWN_ORDER.index((0, 0, KI - 1)):
                        pe.wait_ge(x_hl, e * 4 + 4)
                    if c == k == 0:
                        wait(pe, x_yt, e * 4 + (1 if q == 3 else 0))
                    cols = slice((2 * q + c) * P, (2 * q + c + 1) * P)
                    for w, h in ((whi, hhi), (whi, hlo), (wlo, hhi)):
                        ins = te.matmul(PS[DOWN_BANKS[q]][:, c * C:(c + 1) * C], w[:, k, cols], h[:, k, :],
                                        start=k == 0 and w is whi and h is hhi, stop=k == KI - 1 and w is wlo)
                    if c == 1 and k == KI - 1:
                        ins.then_inc(x_dn, 1)
                rows_transpose(e, 0, after=e + 1 if more else e)
                if not more:
                    rows_transpose(e, 1, after=e)

            expert(0, 0, before=False)
            expert(1, 1)
            with pe.Fori(1, E // 2 - 1) as pair:
                expert(pair * 2, 0)
                expert(pair * 2 + 1, 1)
            expert(E - 2, 0)
            expert(E - 1, 1, more=False)


GROUP_STEPS = 62


def kernel(**inputs):
    import concourse.bacc as bacc
    from concourse.bass_utils import run_bass_kernel_spmd

    a = {k: np.asarray(v) for k, v in inputs.items()}
    T, D = 4096, 1024
    data = {
        "x": a["x"].reshape(T, D),
        "ctx_in": a["ctx_2048"].reshape(T, D),
        "mask": a["mask_Bx1xS2_ff0"].reshape(4, D),
        "router_t": a["L0_ffn_router_w"].T,
        "e_bias": a["L0_ffn_e_bias"],
        "w_gate": a["L0_ffn_W_gate"].reshape(32 * 1024, 512),
        "w_up": a["L0_ffn_W_up"].reshape(32 * 1024, 512),
        "w_down": a["L0_ffn_W_down"].reshape(32 * 512, 1024),
        "sh_gate": a["L0_ffn_shared_gate"].T,
        "sh_up": a["L0_ffn_shared_up"].T,
        "sh_down": a["L0_ffn_shared_down"].T,
    }
    nc = bacc.Bacc("TRN2", target_bir_lowering=False, num_devices=1)
    arrays, args = {}, []
    for name, v in data.items():
        v = np.ascontiguousarray(v)
        arrays[f"in_{name}"] = v
        args.append(nc.dram_tensor(f"in_{name}", v.shape, mybir.dt.from_np(v.dtype), kind="ExternalInput").ap())
    args.append(nc.dram_tensor("out_rows", (T + 160, D), F32, kind="ExternalOutput").ap())
    args.append(nc.dram_tensor("xn_rows", (T, D), F32).ap())
    args.append(nc.dram_tensor("slots", (32 * 160, 2), F32).ap())
    moe_kernel(nc, *args)
    r = run_bass_kernel_spmd(nc, [arrays], core_ids=[0])
    return r.results[0]["out_rows"][:T].reshape(4, 1024, 1024)
```
